# Optimizing a Trainium2 kernel written in Bass

```python
import numpy as np
import jax
import jax.numpy as jnp

def _softmax(x, axis=-1):
    return jax.nn.softmax(x, axis=axis)

def _gelu(x):
    return jax.nn.gelu(x, approximate=True)

def _silu(x):
    return jax.nn.silu(x)

def _sigmoid(x):
    return jax.nn.sigmoid(x)

def _layernorm(x, axis=-1, eps=1e-05):
    m = jnp.mean(x, axis=axis, keepdims=True)
    v = jnp.var(x, axis=axis, keepdims=True)
    return (x - m) / jnp.sqrt(v + eps)

def _scatter_add(tgt, idx, src, axis=0):
    return tgt.at[idx].add(src)

def _segment_sum(src, seg, n):
    return jax.ops.segment_sum(src, seg, n)
kernel_name = 'mk_flamingo_gated_d2_seqx_r8_c51c4e'

def setup_inputs(seed: int=0):
    np.random.seed(seed)
    _w = jnp.asarray

    def _rec_inputs():
        import jax
        import jax.numpy as jnp
        _rk = jax.random.key(seed)
        x = -0.0005207 + 1.001 * jax.random.normal(jax.random.fold_in(_rk, 1), (8, 128, 512), jnp.float32)
        _lenS = 128 - jax.random.randint(jax.random.fold_in(_rk, 7), (8,), 0, max(1, 128 // 4) + 1, jnp.int32)
        _lenS2 = 128 - jax.random.randint(jax.random.fold_in(_rk, 8), (8,), 0, max(1, 128 // 4) + 1, jnp.int32)
        _ctx_4096P = jax.random.normal(jax.random.fold_in(_rk, 11), (8, 16, 512), jnp.float32)
        _ctx_4096c = jax.random.dirichlet(jax.random.fold_in(_rk, 511), 0.3 * jnp.ones((16,), jnp.float32), (8, 128))
        _ctx_4096t = jnp.einsum('bsk,bkd->bsd', _ctx_4096c, _ctx_4096P)
        _ctx_4096t = _ctx_4096t * jax.lax.rsqrt(jnp.mean(jnp.square(_ctx_4096t)) + 1e-12) * 0.953939
        ctx_4096 = -0.00010331 + 0.999899 * (_ctx_4096t + 0.3 * jax.random.normal(jax.random.fold_in(_rk, 611), (8, 128, 512), jnp.float32))
        _g = jax.random.normal(jax.random.fold_in(_rk, 9001), (2, 2), jnp.float32)
        _g = jnp.sign(_g) * jnp.maximum(jnp.abs(_g), 1.0) + (_g == 0) * 1.0
        g_xattn = _g[0]
        g_ffn = _g[1]
        return (x, ctx_4096, g_xattn, g_ffn)
    x, ctx_4096, g_xattn, g_ffn = _rec_inputs()

    def _L0_xattn_setup():
        import jax, jax.numpy as jnp
        import numpy as np
        HEADS = 32
        KV_HEADS = 8
        HEAD_DIM = 128
        EPS = 1e-06

        def rms_norm(x, w):
            var = jnp.mean(jnp.square(x.astype(jnp.float32)), axis=-1, keepdims=True)
            return (x.astype(jnp.float32) * jax.lax.rsqrt(var + EPS)).astype(x.dtype) * w
        key = jax.random.key(seed)
        ks = jax.random.split(key, 6)
        bsz, n_lat, seq, hidden = (8, 64, 512, 512)
        return {'latents': jax.random.normal(ks[0], (bsz, n_lat, hidden), jnp.float32), 'context': jax.random.normal(ks[1], (bsz, seq, hidden), jnp.float32), 'Wq': jax.random.normal(ks[2], (hidden, HEADS * HEAD_DIM), jnp.float32) * 0.02, 'Wk': jax.random.normal(ks[3], (hidden, KV_HEADS * HEAD_DIM), jnp.float32) * 0.02, 'Wv': jax.random.normal(ks[4], (hidden, KV_HEADS * HEAD_DIM), jnp.float32) * 0.02, 'Wo': jax.random.normal(ks[5], (HEADS * HEAD_DIM, hidden), jnp.float32) * 0.02, 'q_norm_w': jnp.ones((HEAD_DIM,), jnp.float32), 'k_norm_w': jnp.ones((HEAD_DIM,), jnp.float32)}
    _L0_xattn_all = _L0_xattn_setup()
    _L0_xattn_in = {k: v for k, v in _L0_xattn_all.items() if k in ('Wq', 'Wk', 'Wv', 'Wo', 'q_norm_w', 'k_norm_w')}
    del _L0_xattn_all

    def _L0_ffn_setup():
        import jax, jax.numpy as jnp
        import numpy as np
        ALPHA = 32
        R = 16
        SCALING = ALPHA / R
        key = jax.random.key(seed)
        k1, k2, k3, k4 = jax.random.split(key, 4)
        B_, S, D = (4, 256, 512)
        H, r, O = (8, R, 512)
        x = jax.random.normal(k1, (B_, S, D), dtype=jnp.float32)
        A = jax.random.normal(k2, (H, r, D), dtype=jnp.float32) * 0.02
        Bm = jax.random.normal(k3, (H, O, r), dtype=jnp.float32) * 0.02
        Wr = jax.random.normal(k4, (H, D), dtype=jnp.float32) * 0.02
        br = jnp.zeros((H,), dtype=jnp.float32)
        return {'x': x, 'A': A, 'B': Bm, 'Wr': Wr, 'br': br}
    _L0_ffn_all = _L0_ffn_setup()
    _L0_ffn_in = {k: v for k, v in _L0_ffn_all.items() if k in ('A', 'B', 'Wr', 'br')}
    del _L0_ffn_all

    def _L1_xattn_setup():
        import jax, jax.numpy as jnp
        import numpy as np
        B, Q, D = (8, 64, 512)
        CTX = 512
        H, KV, HD = (16, 4, 96)
        G = H // KV
        key = jax.random.key(seed)
        ks = jax.random.split(key, 6)
        s = 0.02
        return {'latents': jax.random.normal(ks[0], (B, Q, D), jnp.float32), 'context': jax.random.normal(ks[1], (B, CTX, D), jnp.float32), 'Wq': jax.random.normal(ks[2], (H * HD, D), jnp.float32) * s, 'Wk': jax.random.normal(ks[3], (KV * HD, D), jnp.float32) * s, 'Wv': jax.random.normal(ks[4], (KV * HD, D), jnp.float32) * s, 'Wo': jax.random.normal(ks[5], (D, H * HD), jnp.float32) * s}
    _L1_xattn_all = _L1_xattn_setup()
    _L1_xattn_in = {k: v for k, v in _L1_xattn_all.items() if k in ('Wq', 'Wk', 'Wv', 'Wo')}
    del _L1_xattn_all

    def _L1_ffn_setup():
        import jax, jax.numpy as jnp
        import numpy as np
        HD, M = (512, 1792)
        key = jax.random.key(seed)
        k_x, k_g, k_u, k_d = jax.random.split(key, 4)
        scale = 1.0 / np.sqrt(HD)
        x = jax.random.normal(k_x, (4, 256, HD), dtype=jnp.float16)
        W_gate = jax.random.normal(k_g, (M, HD), dtype=jnp.float16) * jnp.float16(scale)
        W_up = jax.random.normal(k_u, (M, HD), dtype=jnp.float16) * jnp.float16(scale)
        W_down = jax.random.normal(k_d, (HD, M), dtype=jnp.float16) * jnp.float16(1.0 / np.sqrt(M))
        return {'x': x, 'W_gate': W_gate, 'W_up': W_up, 'W_down': W_down}
    _L1_ffn_all = _L1_ffn_setup()
    _L1_ffn_in = {k: v for k, v in _L1_ffn_all.items() if k in ('W_gate', 'W_up', 'W_down')}
    del _L1_ffn_all
    return {'x': x, 'ctx_4096': ctx_4096, 'g_xattn': g_xattn, 'g_ffn': g_ffn, 'L0_xattn_Wq': _L0_xattn_in['Wq'], 'L0_xattn_Wk': _L0_xattn_in['Wk'], 'L0_xattn_Wv': _L0_xattn_in['Wv'], 'L0_xattn_Wo': _L0_xattn_in['Wo'], 'L0_xattn_q_norm_w': _L0_xattn_in['q_norm_w'], 'L0_xattn_k_norm_w': _L0_xattn_in['k_norm_w'], 'L0_ffn_A': _L0_ffn_in['A'], 'L0_ffn_B': _L0_ffn_in['B'], 'L0_ffn_Wr': _L0_ffn_in['Wr'], 'L0_ffn_br': _L0_ffn_in['br'], 'L1_xattn_Wq': _L1_xattn_in['Wq'], 'L1_xattn_Wk': _L1_xattn_in['Wk'], 'L1_xattn_Wv': _L1_xattn_in['Wv'], 'L1_xattn_Wo': _L1_xattn_in['Wo'], 'L1_ffn_W_gate': _L1_ffn_in['W_gate'], 'L1_ffn_W_up': _L1_ffn_in['W_up'], 'L1_ffn_W_down': _L1_ffn_in['W_down']}

def reference(x, ctx_4096, g_xattn, g_ffn, L0_xattn_Wq, L0_xattn_Wk, L0_xattn_Wv, L0_xattn_Wo, L0_xattn_q_norm_w, L0_xattn_k_norm_w, L0_ffn_A, L0_ffn_B, L0_ffn_Wr, L0_ffn_br, L1_xattn_Wq, L1_xattn_Wk, L1_xattn_Wv, L1_xattn_Wo, L1_ffn_W_gate, L1_ffn_W_up, L1_ffn_W_down):
    import jax
    import jax.numpy as jnp

    def _L0_xattn_ref(latents, context, Wq, Wk, Wv, Wo, q_norm_w, k_norm_w):
        import jax, jax.numpy as jnp
        import numpy as np
        HEADS = 32
        KV_HEADS = 8
        HEAD_DIM = 128
        EPS = 1e-06

        def rms_norm(x, w):
            var = jnp.mean(jnp.square(x.astype(jnp.float32)), axis=-1, keepdims=True)
            return (x.astype(jnp.float32) * jax.lax.rsqrt(var + EPS)).astype(x.dtype) * w
        bsz, q_len, hidden = latents.shape
        kv = jnp.concatenate([context, latents], axis=1)
        kv_len = kv.shape[1]
        groups = HEADS // KV_HEADS
        q = (latents @ Wq).reshape(bsz, q_len, HEADS, HEAD_DIM).transpose(0, 2, 1, 3)
        k = (kv @ Wk).reshape(bsz, kv_len, KV_HEADS, HEAD_DIM).transpose(0, 2, 1, 3)
        v = (kv @ Wv).reshape(bsz, kv_len, KV_HEADS, HEAD_DIM).transpose(0, 2, 1, 3)
        q = rms_norm(q, q_norm_w)
        k = rms_norm(k, k_norm_w)
        qg = q.reshape(bsz, KV_HEADS, groups, q_len, HEAD_DIM)
        scale = 1.0 / np.sqrt(HEAD_DIM)
        scores = jnp.einsum('bhgqd,bhkd->bhgqk', qg, k) * scale
        probs = jax.nn.softmax(scores.astype(jnp.float32), axis=-1).astype(q.dtype)
        out = jnp.einsum('bhgqk,bhkd->bhgqd', probs, v)
        out = out.reshape(bsz, HEADS, q_len, HEAD_DIM).transpose(0, 2, 1, 3)
        out = out.reshape(bsz, q_len, HEADS * HEAD_DIM)
        return out @ Wo

    def _L0_ffn_ref(x, A, B, Wr, br):
        import jax, jax.numpy as jnp
        import numpy as np
        ALPHA = 32
        R = 16
        SCALING = ALPHA / R
        H = A.shape[0]
        router_logits = jnp.einsum('bsd,hd->bsh', x, Wr) + br
        scores = H * jax.nn.softmax(router_logits, axis=-1)
        low = jnp.einsum('bsd,hrd->bshr', x, A)
        out = jnp.einsum('bshr,hor,bsh->bso', low, B, scores)
        return SCALING * out

    def _L1_xattn_ref(latents, context, Wq, Wk, Wv, Wo):
        import jax, jax.numpy as jnp
        import numpy as np
        B, Q, D = (8, 64, 512)
        CTX = 512
        H, KV, HD = (16, 4, 96)
        G = H // KV
        b, q_len, _ = latents.shape
        hidden = jnp.concatenate([context, latents], axis=1)
        s_len = hidden.shape[1]
        q = (latents @ Wq.T).reshape(b, q_len, H, HD)
        k = (hidden @ Wk.T).reshape(b, s_len, KV, HD)
        v = (hidden @ Wv.T).reshape(b, s_len, KV, HD)
        q = q.transpose(0, 2, 1, 3).reshape(b, KV, G, q_len, HD)
        k = k.transpose(0, 2, 1, 3)
        v = v.transpose(0, 2, 1, 3)
        scale = 1.0 / jnp.sqrt(jnp.asarray(HD, q.dtype))
        scores = jnp.einsum('bkgqd,bksd->bkgqs', q, k) * scale
        attn = jax.nn.softmax(scores.astype(jnp.float32), axis=-1).astype(q.dtype)
        out = jnp.einsum('bkgqs,bksd->bkgqd', attn, v)
        out = out.reshape(b, H, q_len, HD).transpose(0, 2, 1, 3).reshape(b, q_len, H * HD)
        return out @ Wo.T

    def _L1_ffn_ref(x, W_gate, W_up, W_down):
        import jax, jax.numpy as jnp
        import numpy as np
        HD, M = (512, 1792)
        gate = jnp.einsum('bsh,mh->bsm', x, W_gate)
        up = jnp.einsum('bsh,mh->bsm', x, W_up)
        h = jax.nn.silu(gate) * up
        out = jnp.einsum('bsm,hm->bsh', h, W_down)
        return out
    x = x + jnp.tanh(g_xattn[0]) * _L0_xattn_ref(_layernorm(x, axis=-1), ctx_4096, L0_xattn_Wq, L0_xattn_Wk, L0_xattn_Wv, L0_xattn_Wo, L0_xattn_q_norm_w, L0_xattn_k_norm_w)
    x = x + jnp.tanh(g_ffn[0]) * _L0_ffn_ref(_layernorm(x, axis=-1), L0_ffn_A, L0_ffn_B, L0_ffn_Wr, L0_ffn_br)
    x = x + jnp.tanh(g_xattn[1]) * _L1_xattn_ref(_layernorm(x, axis=-1), ctx_4096, L1_xattn_Wq, L1_xattn_Wk, L1_xattn_Wv, L1_xattn_Wo)
    x = x + jnp.tanh(g_ffn[1]) * _L1_ffn_ref(_layernorm(x, axis=-1), L1_ffn_W_gate, L1_ffn_W_up, L1_ffn_W_down)
    return x

_drawn_inputs = setup_inputs


def setup_inputs(seed=0):
    import zlib

    import numpy as np

    out = dict(_drawn_inputs(seed))
    spreads = {'g_ffn': (-1.0, 0.2),
     'L0_xattn_q_norm_w': (1.0, 0.6),
     'L0_xattn_k_norm_w': (1.0, 0.6),
     'L0_ffn_br': (0.0, 0.1)}
    factors = {'L1_xattn_Wq': 5.928, 'L1_xattn_Wk': 5.97}
    for name, (base, spread) in spreads.items():
        noise = np.random.default_rng([zlib.crc32(name.encode()), seed]).standard_normal(out[name].shape)
        drawn = base * np.exp(spread * noise) if base else spread * noise
        out[name] = jnp.asarray(drawn.astype(out[name].dtype))
    for name, factor in factors.items():
        out[name] = (out[name] * factor).astype(out[name].dtype)
    return out
```

```python
from contextlib import ExitStack

import concourse.bass as bass
from concourse import mybir

F32 = mybir.dt.float32
F32R = mybir.dt.float32r
ALU = mybir.AluOpType
ACT = mybir.ActivationFunctionType
AX = mybir.AxisListType

P = 128
BATCH, SEQ, D = 8, 128, 512
KC = D // P
NT = BATCH
TOK = BATCH * SEQ
NH = 4
NB = 4
HALF = NB * SEQ
VS = 4
KV = 2 * SEQ
LN_EPS = 1e-5
RMS_EPS = 1e-6
EXPERTS, RANK = 8, 16
LORA_GAIN = EXPERTS * 2.0
FF = 1792
MT = FF // P


class Layer:

    def __init__(self, name, groups, head_dim, normed, gate):
        self.name, self.groups, self.hd, self.normed, self.gate = name, groups, head_dim, normed, gate
        self.qw = NH * head_dim
        self.kvw = 2 * head_dim


L0 = Layer("a", 8, 128, True, 0)
L1 = Layer("c", 4, 96, False, 1)


class AttentionSems:

    def __init__(self, sem):
        self.in_q = sem("in_q")
        self.in_kv = sem("in_kv")
        self.in_o = sem("in_o")
        self.wq_hi = sem("wq_hi")
        self.wq_lo = sem("wq_lo")
        self.wkv_hi = sem("wkv_hi")
        self.wkv_lo = sem("wkv_lo")
        self.wo_hi = sem("wo_hi")
        self.wo_lo = sem("wo_lo")
        self.q_done = sem("q_done")
        self.qsq_done = sem("qsq_done")
        self.qcp_done = sem("qcp_done")
        self.qt_done = sem("qt_done")
        self.qthi_done = sem("qthi_done")
        self.qlo_done = sem("qlo_done")
        self.qvar_done = sem("qvar_done")
        self.rq_done = sem("rq_done")
        self.kv_done = sem("kv_done")
        self.ksq_done = sem("ksq_done")
        self.kvar_done = sem("kvar_done")
        self.kr_done = sem("kr_done")
        self.vhi_done = sem("vhi_done")
        self.vlo_done = sem("vlo_done")
        self.kn_done = sem("kn_done")
        self.kt_done = sem("kt_done")
        self.khi_done = sem("khi_done")
        self.klo_done = sem("klo_done")
        self.s_done = sem("s_done")
        self.mx_done = sem("mx_done")
        self.nb_done = sem("nb_done")
        self.exp_done = sem("exp_done")
        self.rs_done = sem("rs_done")
        self.pn_done = sem("pn_done")
        self.t_done = sem("t_done")
        self.pthi_done = sem("pthi_done")
        self.ptlo_done = sem("ptlo_done")
        self.pv_done = sem("pv_done")
        self.ohi_done = sem("ohi_done")
        self.olo_done = sem("olo_done")
        self.y_done = sem("y_done")
        self.yadd_done = sem("yadd_done")


def count(g, b, per_tile, more):
    return g * (NT * per_tile) + (b * per_tile + more)


def build(nc, a):
    with ExitStack() as ctx:
        def sb(name, n, dt=F32):
            return ctx.enter_context(nc.sbuf_tensor(name, [P, n], dt))

        def sem(name):
            return ctx.enter_context(nc.semaphore(name))

        split = sb("split", 38912, F32R)
        spot = [0]

        def take(n):
            spot[0] += n
            return split[:, spot[0] - n:spot[0]]

        def chunks(ap, n):
            return ap.rearrange("p (k n) -> p k n", k=n)

        def pair(n, k):
            return chunks(take(n), k), chunks(take(n), k)

        xT = pair(KC * TOK, KC)
        cT = pair(KC * TOK, KC)
        weights_at = spot[0]
        wq = pair(KC * 512, KC)
        wkv = pair(KC * 256, KC)
        wo = pair(NH * 512, NH)
        kT = [pair(KV, 1) for _ in range(2)]
        v = [pair(2 * P, 2) for _ in range(VS)]
        qT = [pair(NH * P, NH) for _ in range(2)]
        pT = pair(2 * NH * P, 2)
        oT = pair(NH * P, NH)
        assert spot[0] <= 38912

        spot[0] = weights_at
        lw = pair(KC * 136, KC)
        lb = pair(D, 1)
        tT = pair(P, 1)
        spot[0] = 2 * KC * TOK
        fgate = chunks(take(KC * FF), KC)
        fup = chunks(take(KC * FF), KC)
        fdown = chunks(take(MT * D), MT)
        hT = [pair(HALF, 1) for _ in range(2)]
        assert spot[0] <= 38912

        x = sb("x", NT * D)
        xt = x[:, :].rearrange("p (t d) -> p t d", t=NT)
        raw = sb("raw", 5120)
        raw_q = raw[:, 0:2048]
        raw_kv = raw[:, 2048:3072]
        raw_o = raw[:, 3072:5120]
        scratch = sb("scratch", 4096)
        craw = scratch[:, :].rearrange("p (k n) -> p k n", k=KC)
        probs = scratch[:, 0:1024].rearrange("p (h n) -> p h n", h=NH)
        qn = scratch[:, 1024:1536]
        kn = scratch[:, 1536:1792]
        sink = [scratch[:, 1792 + P * i:1792 + P * (i + 1)] for i in range(6)]
        xn = [scratch[:, 2560 + 512 * i:3072 + 512 * i] for i in range(2)]
        lora_act = [scratch[:, P * i:P * (i + 1)] for i in range(2)]
        sig = [scratch[:, 0 + 512 * i:512 + 512 * i] for i in range(2)]
        gated = [scratch[:, 1024 + 512 * i:1536 + 512 * i] for i in range(2)]
        hidden = [scratch[:, 2048 + 512 * i:2560 + 512 * i] for i in range(2)]

        ident = sb("ident", P)
        half_neg = sb("half_neg", 16)
        gates = sb("gates", 4)
        tg = sb("tg", 4)
        tg_lora = sb("tg_lora", 1)
        qkw = sb("qkw", 3)
        bias_r = sb("bias_r", EXPERTS)
        stats = sb("stats", NT * 6)
        moments = sb("moments", NT * 2)
        var_e = sb("var_e", NT)
        rstd = sb("rstd", NT)
        ksum = sb("ksum", 4)
        kvar = sb("kvar", 4)
        kr = sb("kr", 4)
        qsum = sb("qsum", 8)
        qvar = sb("qvar", 8)
        rq = sb("rq", 8)
        hd_eps = sb("hd_eps", 4)
        mx = sb("mx", NH)
        nb = sb("nb", NH)
        sums = sb("sums", NH)
        rs = sb("rs", NH)
        lg = sb("lg", 2 * EXPERTS)
        lmx = sb("lmx", 2)
        lsum = sb("lsum", 2)
        lrs = sb("lrs", 2)

        bank = [ctx.enter_context(nc.psum_tensor(f"bank{i}", [P, 512], F32)) for i in range(8)]

        in_x, in_ctx, in_small, in_lora = sem("in_x"), sem("in_ctx"), sem("in_small"), sem("in_lora")
        in_ffw = sem("in_ffw")
        ident_zero, consts = sem("ident_zero"), sem("consts")
        tanh_done, gate_done, qkw_done = sem("tanh_done"), sem("gate_done"), sem("qkw_done")
        chi_done, clo_done = sem("chi_done"), sem("clo_done")
        ln_stats, ln_moments, ln_vareps = sem("ln_stats"), sem("ln_moments"), sem("ln_vareps")
        ln_rstd, ln_xn, ln_t, ln_hi, ln_lo = (sem(f"ln_{n}") for n in ("rstd", "xn", "t", "hi", "lo"))
        out_done = sem("out_done")

        attn_sems = {L.name: AttentionSems(lambda what, L=L: sem(f"{L.name}_{what}")) for L in (L0, L1)}
        lw_hi, lw_lo, lo_p, lo_mx = sem("lw_hi"), sem("lw_lo"), sem("lo_p"), sem("lo_mx")
        lo_lg, lo_exp, lo_rs, lo_sc, lo_t = sem("lo_lg"), sem("lo_exp"), sem("lo_rs"), sem("lo_sc"), sem("lo_t")
        lo_tr, lo_thi, lo_tlo, lo_y, lo_add = sem("lo_tr"), sem("lo_thi"), sem("lo_tlo"), sem("lo_y"), sem("lo_add")
        ff_g, ff_sig, ff_u, ff_gated, ff_h = sem("ff_g"), sem("ff_sig"), sem("ff_u"), sem("ff_gated"), sem("ff_h")
        ff_hhi, ff_hlo, ff_acc, ff_add = sem("ff_hhi"), sem("ff_hlo"), sem("ff_acc"), sem("ff_add")

        def q_src(L, g):
            w = a["wq_" + L.name].rearrange("(k p) n -> p k n", p=P)
            return w[:, :, bass.ds(g * L.qw, L.qw)]

        def kv_src(L, g, which):
            w = a[which + L.name].rearrange("(k p) n -> p k n", p=P)
            return w[:, :, bass.ds(g * L.hd, L.hd)]

        def o_src(L, g):
            w = a["wo_" + L.name].rearrange("(n p) m -> p n m", p=L.hd)
            return w[:, bass.ds(g * NH, NH), :]

        def rawq(L):
            return raw_q[:, 0:KC * L.qw].rearrange("p (k n) -> p k n", k=KC)

        def rawkv(L):
            return raw_kv[:, 0:KC * L.kvw].rearrange("p (k n) -> p k n", k=KC)

        def rawo(L):
            return raw_o[0:L.hd, :].rearrange("p (k n) -> p k n", k=NH)

        def flat(w):
            return w.rearrange("p k n -> p (k n)")

        block = ctx.enter_context(nc.Block())

        def groups(eng, L, body):
            body(0, True, False)
            with eng.Fori(1, L.groups - 1) as g:
                body(g, False, False)
            body(L.groups - 1, False, True)

        def of(g, b):
            return (g + b // NT, b % NT)

        @block.sync
        def _(sp):
            sp.dma_start(xt, a["x"].rearrange("(t p) d -> p t d", p=P)).then_inc(in_x, 16)
            sp.dma_start(craw, a["ctx_t"].rearrange("(k p) n -> p k n", p=P)).then_inc(in_ctx, 16)
            for n, name in enumerate(("g_xattn", "g_ffn")):
                sp.dma_start(gates[:, 2 * n:2 * n + 2], a[name].partition_broadcast(P)).then_inc(in_small, 16)
            sp.dma_start(qkw[:, 0:1], a["q_norm_w"].rearrange("(p a) -> p a", a=1)).then_inc(in_small, 16)
            sp.dma_start(qkw[:, 1:2], a["k_norm_w"].rearrange("(p a) -> p a", a=1)).then_inc(in_small, 16)
            sp.dma_start(bias_r[:, :], a["lora_bias"].partition_broadcast(P)).then_inc(in_small, 16)

            def load_q(L, g):
                sp.dma_start(rawq(L), q_src(L, g)).then_inc(attn_sems[L.name].in_q, 16)

            def load_kv(L, g):
                s = attn_sems[L.name]
                sp.dma_start(rawkv(L)[:, :, 0:L.hd], kv_src(L, g, "wk_")).then_inc(s.in_kv, 16)
                sp.dma_start(rawkv(L)[:, :, L.hd:L.kvw], kv_src(L, g, "wv_")).then_inc(s.in_kv, 16)

            def load_o(L, g):
                sp.dma_start(rawo(L), o_src(L, g)).then_inc(attn_sems[L.name].in_o, 16)

            def layer(L):
                s = attn_sems[L.name]
                load_q(L, 0)
                load_kv(L, 0)
                load_o(L, 0)

                def next_group(g):
                    sp.wait_ge(s.wq_lo, g * KC)
                    load_q(L, g)
                    sp.wait_ge(s.wkv_lo, g * 2)
                    load_kv(L, g)
                    sp.wait_ge(s.wo_lo, g * NH)
                    load_o(L, g)

                with sp.Fori(1, L.groups) as g:
                    next_group(g)

            layer(L0)
            s = attn_sems[L0.name]
            sp.wait_ge(s.wq_lo, L0.groups * KC)
            sp.wait_ge(s.wkv_lo, L0.groups * 2)
            sp.dma_start(raw_q[:, 0:KC * 136].rearrange("p (k n) -> p k n", k=KC),
                         a["lora_w"].rearrange("(k p) n -> p k n", p=P)).then_inc(in_lora, 16)
            sp.dma_start(raw_kv[:, 0:D], a["lora_b"]).then_inc(in_lora, 16)
            sp.wait_ge(lw_lo, 2)
            sp.wait_ge(s.wo_lo, L0.groups * NH)
            layer(L1)
            sp.wait_ge(ff_add, 2 * NB)
            sp.dma_start(a["out"].rearrange("(t p) d -> p t d", p=P), xt).then_inc(out_done, 16)
            sp.wait_ge(out_done, 16)

        @block.tensor
        def _(pe):
            def mm3(out, w, m, start=False, stop=False, wat=None, mat=None):
                whi, wlo = w
                mhi, mlo = m
                pe.matmul(out, whi, mhi, start=start, stop=False)
                pe.matmul(out, whi, mlo, start=False, stop=False)
                return pe.matmul(out, wlo, mhi, start=False, stop=stop)

            def at(pr, *idx):
                return tuple(t[idx] for t in pr)

            def layer_norm(n):
                for t in range(NT):
                    pe.wait_ge(ln_xn, n * NT + t + 1)
                    if t >= 2:
                        pe.wait_ge(ln_lo, n * NT + t - 1)
                    b = bank[6 + t % 2]
                    for k in range(KC):
                        last = pe.transpose(b[:, k * P:(k + 1) * P], xn[t % 2][:, k * P:(k + 1) * P], ident[:, :])
                    last.then_inc(ln_t, 1)

            def attention(L):
                s = attn_sems[L.name]
                hd = L.hd

                def cols(w, k, n):
                    return tuple(flat(t)[:, k * n:(k + 1) * n] for t in w)

                def kv_proj(g, b):
                    gb, tile = of(g, b)
                    if tile == 0:
                        pe.wait_ge(s.wkv_lo, gb * 2 + 2)
                    if not (isinstance(g, int) and g == b == 0):
                        pe.wait_ge(s.klo_done, count(g, b, 1, 0))
                    for i, src in enumerate((cT, xT)):
                        out = bank[7][:, i * L.kvw:(i + 1) * L.kvw]
                        for k in range(KC):
                            last = mm3(out, at(src, slice(None), k, slice(tile * P, (tile + 1) * P)),
                                       cols(wkv, k, L.kvw), start=k == 0, stop=k == KC - 1)
                    last.then_inc(s.kv_done, 1)

                def q_proj(g, b):
                    gb, tile = of(g, b)
                    if tile == 0:
                        pe.wait_ge(s.wq_lo, gb * KC + KC)
                    if not (isinstance(g, int) and g == b == 0):
                        pe.wait_ge(s.qlo_done, count(g, b, 1, 0))
                    for k in range(KC):
                        last = mm3(bank[6][:, 0:L.qw], at(xT, slice(None), k, slice(tile * P, (tile + 1) * P)),
                                   cols(wq, k, L.qw), start=k == 0, stop=k == KC - 1)
                    last.then_inc(s.q_done, 1)

                def k_turn(g, b):
                    pe.wait_ge(s.kn_done, count(g, b, 2, 2))
                    for i in range(2):
                        last = pe.transpose(bank[7][0:hd, i * P:(i + 1) * P], kn[:, i * hd:(i + 1) * hd],
                                            ident[:, :])
                    last.then_inc(s.kt_done, 1)

                def q_turn(g, b):
                    pe.wait_ge(s.qcp_done, count(g, b, 1, 1))
                    for h in range(NH):
                        last = pe.transpose(bank[6][0:hd, h * P:(h + 1) * P], qn[:, h * hd:(h + 1) * hd],
                                            ident[:, :])
                    last.then_inc(s.qt_done, 1)

                def scores(g, b):
                    pe.wait_ge(s.klo_done, count(g, b, 1, 1))
                    pe.wait_ge(s.qlo_done, count(g, b, 1, 1))
                    for h in range(NH):
                        last = mm3(bank[h // 2][:, (h % 2) * KV:(h % 2 + 1) * KV],
                                   at(qT[b % 2], slice(0, hd), h, slice(None)),
                                   at(kT[b % 2], slice(0, hd), 0, slice(None)), start=True, stop=True)
                        if h % 2:
                            last.then_inc(s.s_done, 1)

                def turn(g, b):
                    for i in range(2):
                        pe.wait_ge(s.pn_done, count(g, b, NH, 2 * i + 2))
                        for kt in range(2):
                            for h in (2 * i, 2 * i + 1):
                                last = pe.transpose(bank[2 + kt][:, h * P:(h + 1) * P],
                                                    probs[:, h, kt * P:(kt + 1) * P], ident[:, :])
                            if i == 1:
                                last.then_inc(s.t_done, 1)

                def values(g, b):
                    for kt in range(2):
                        pe.wait_ge(s.ptlo_done, count(g, b, 2, kt + 1))
                        last = mm3(bank[4][0:hd, :],
                                   tuple(flat(w)[:, kt * hd:(kt + 1) * hd] for w in v[b % VS]),
                                   at(pT, slice(None), kt, slice(None)), start=kt == 0, stop=kt == 1)
                    last.then_inc(s.pv_done, 1)

                def project(g, b):
                    pe.wait_ge(s.olo_done, count(g, b, 1, 1))
                    if b == 0:
                        pe.wait_ge(s.wo_lo, g * NH + NH)
                    if not (isinstance(g, int) and g == b == 0):
                        pe.wait_ge(s.yadd_done, count(g, b, 1, 0))
                    for h in range(NH):
                        last = mm3(bank[5][:, :], at(oT, slice(0, hd), h, slice(None)),
                                   at(wo, slice(0, hd), h, slice(None)), start=h == 0, stop=h == NH - 1)
                    last.then_inc(s.y_done, 1)

                def body(g, first, last):
                    for b in range(NT):
                        ahead = not last or b + 2 < NT
                        turn(g, b)
                        if ahead:
                            kv_proj(g, b + 2)
                        values(g, b)
                        if not last or b + 1 < NT:
                            scores(g, b + 1)
                        if ahead:
                            q_proj(g, b + 2)
                            k_turn(g, b + 2)
                        project(g, b)
                        if ahead:
                            q_turn(g, b + 2)

                for b in range(2):
                    kv_proj(0, b)
                    q_proj(0, b)
                    k_turn(0, b)
                    q_turn(0, b)
                scores(0, 0)
                groups(pe, L, body)

            pe.wait_ge(consts, 3)
            layer_norm(0)
            pe.wait_ge(ln_lo, NT)
            pe.wait_ge(clo_done, KC)
            attention(L0)

            layer_norm(1)
            pe.wait_ge(lw_lo, 2)
            pe.wait_ge(ln_lo, 2 * NT)
            for t in range(NT + 1):
                if t < NT:
                    if t >= 2:
                        pe.wait_ge(lo_t, t - 1)
                    for k in range(KC):
                        last = mm3(bank[6 + t % 2][:, 0:136], at(xT, slice(None), k, slice(t * P, (t + 1) * P)),
                                   at(lw, slice(None), k, slice(None)), start=k == 0, stop=k == KC - 1)
                    last.then_inc(lo_p, 1)
                if t >= 1:
                    n = t - 1
                    pe.wait_ge(lo_t, n + 1)
                    pe.transpose(bank[2][:, 0:P], lora_act[n % 2], ident[:, :]).then_inc(lo_tr, 1)
                    pe.wait_ge(lo_tlo, n + 1)
                    if n >= 2:
                        pe.wait_ge(lo_add, n - 1)
                    mm3(bank[4 + n % 2][:, :], at(tT, slice(None), 0, slice(None)),
                        at(lb, slice(None), 0, slice(None)), start=True, stop=True).then_inc(lo_y, 1)

            layer_norm(2)
            pe.wait_ge(ln_lo, 3 * NT)
            attention(L1)

            layer_norm(3)
            pe.wait_ge(ln_lo, 4 * NT)
            pe.wait_ge(in_ffw, 48)
            with pe.Fori(0, 2) as half:
                toks = bass.ds(half * HALF, HALF)

                def down(m):
                    pe.wait_ge(ff_hlo, half * MT + (m + 1))
                    for t in range(NB):
                        for i, part in enumerate(hT[m % 2]):
                            last = pe.matmul(bank[t][:, :], part[:, 0, t * P:(t + 1) * P], fdown[:, m, :],
                                             start=m == 0 and i == 0, stop=m == MT - 1 and i == 1)
                    last.then_inc(ff_acc, 1)

                for m in range(MT):
                    for w, bk, done in ((fgate, 4, ff_g), (fup, 6, ff_u)):
                        if m >= 2:
                            pe.wait_ge(ff_h, half * MT + (m - 1))
                        for k in range(KC):
                            for i, part in enumerate(xT):
                                last = pe.matmul(bank[bk + m % 2][:, :], w[:, k, m * P:(m + 1) * P],
                                                 part[:, k, toks],
                                                 start=k == 0 and i == 0, stop=k == KC - 1 and i == 1)
                        last.then_inc(done, 1)
                    if m >= 1:
                        down(m - 1)
                down(MT - 1)
                pe.wait_ge(ff_add, half * NB + NB)

        @block.scalar
        def _(act):
            def copy(out, in_):
                return act.activation(out, in_, ACT.Copy)

            def layer_norm(n):
                for t in range(NT):
                    act.wait_ge(ln_t, n * NT + t + 1)
                    copy(xT[0][:, :, t * P:(t + 1) * P],
                         bank[6 + t % 2][:, :].rearrange("p (k n) -> p k n", k=KC)).then_inc(ln_hi, 1)

            def attention(L):
                s = attn_sems[L.name]
                hd = L.hd

                def kv_evac(g, b):
                    act.wait_ge(s.kv_done, count(g, b, 1, 1))
                    ps = bank[7]
                    if L.normed:
                        for i in range(2):
                            act.activation(sink[i], ps[:, i * L.kvw:i * L.kvw + hd], ACT.Square,
                                           accum_out=ksum[:, 2 * (b % 2) + i:2 * (b % 2) + i + 1]
                                           ).then_inc(s.ksq_done, 1)
                    copy(flat(v[b % VS][0])[:, 0:2 * hd].rearrange("p (t n) -> p t n", t=2),
                         ps[:, 0:2 * L.kvw].rearrange("p (t n) -> p t n", t=2)[:, :, hd:L.kvw]
                         ).then_inc(s.vhi_done, 1)

                def q_evac(g, b):
                    act.wait_ge(s.q_done, count(g, b, 1, 1))
                    if L.normed:
                        for h in range(NH):
                            act.activation(sink[2 + h], bank[6][:, h * hd:(h + 1) * hd], ACT.Square,
                                           accum_out=qsum[:, NH * (b % 2) + h:NH * (b % 2) + h + 1]
                                           ).then_inc(s.qsq_done, 1)
                    copy(qn[:, 0:L.qw], bank[6][:, 0:L.qw]).then_inc(s.qcp_done, 1)

                def k_evac(g, b):
                    act.wait_ge(s.kt_done, count(g, b, 1, 1))
                    out, ps = kT[b % 2][0][0:hd, 0, :], bank[7][0:hd, 0:KV]
                    if L.normed:
                        act.activation(out, ps, ACT.Copy, scale=qkw[:, 2:3]).then_inc(s.khi_done, 1)
                    else:
                        copy(out, ps).then_inc(s.khi_done, 1)

                def qt_evac(g, b):
                    act.wait_ge(s.qt_done, count(g, b, 1, 1))
                    copy(flat(qT[b % 2][0])[0:hd, :], bank[6][0:hd, :]).then_inc(s.qthi_done, 1)

                def exps(g, b):
                    for h in range(NH):
                        if h % 2 == 0:
                            act.wait_ge(s.nb_done, count(g, b, 2, h // 2 + 1))
                        scale = rq[:, NH * (b % 2) + h:NH * (b % 2) + h + 1] if L.normed else float(hd) ** -0.5
                        act.activation(probs[:, h, :], bank[h // 2][:, (h % 2) * KV:(h % 2 + 1) * KV], ACT.Exp,
                                       bias=nb[:, h:h + 1], scale=scale,
                                       accum_out=sums[:, h:h + 1]).then_inc(s.exp_done, 1)

                def turn_evac(g, b):
                    for kt in range(2):
                        act.wait_ge(s.t_done, count(g, b, 2, kt + 1))
                        copy(pT[0][:, kt, :], bank[2 + kt][:, :]).then_inc(s.pthi_done, 1)

                def o_evac(g, b):
                    act.wait_ge(s.pv_done, count(g, b, 1, 1))
                    copy(flat(oT[0])[0:hd, :], bank[4][0:hd, :]).then_inc(s.ohi_done, 1)

                def kv_hi(g):
                    act.wait_ge(s.in_kv, g * 32 + 32)
                    for i in range(2):
                        sl = slice(i * 2 * L.kvw, (i + 1) * 2 * L.kvw)
                        copy(flat(wkv[0])[:, sl], raw_kv[:, sl]).then_inc(s.wkv_hi, 1)

                def q_hi(g):
                    act.wait_ge(s.in_q, g * 16 + 16)
                    for k in range(KC):
                        sl = slice(k * L.qw, (k + 1) * L.qw)
                        copy(flat(wq[0])[:, sl], raw_q[:, sl]).then_inc(s.wq_hi, 1)

                def o_hi(g):
                    act.wait_ge(s.in_o, g * 16 + 16)
                    for h in range(NH):
                        copy(wo[0][0:hd, h, :], rawo(L)[:, h, :]).then_inc(s.wo_hi, 1)

                def body(g, first, last):
                    for b in range(NT):
                        ahead = not last or b + 2 < NT
                        turn_evac(g, b)
                        if b == 0 and not first:
                            act.wait_ge(s.y_done, count(g, 0, 1, 0))
                            o_hi(g)
                        if ahead:
                            kv_evac(g, b + 2)
                            if b + 2 == NT - 1 and not last:
                                kv_hi(g + 1)
                        o_evac(g, b)
                        if not last or b + 1 < NT:
                            exps(g, b + 1)
                        if ahead:
                            q_evac(g, b + 2)
                            if b + 2 == NT - 1 and not last:
                                q_hi(g + 1)
                            k_evac(g, b + 2)
                            qt_evac(g, b + 2)

                kv_hi(0)
                q_hi(0)
                o_hi(0)
                for b in range(2):
                    kv_evac(0, b)
                    q_evac(0, b)
                    k_evac(0, b)
                    qt_evac(0, b)
                exps(0, 0)
                groups(act, L, body)

            act.wait_ge(in_small, 80)
            act.activation(tg[:, :], gates[:, :], ACT.Tanh).then_inc(tanh_done, 1)
            for k in range(KC):
                act.wait_ge(in_ctx, 16)
                copy(cT[0][:, k, :], craw[:, k, :]).then_inc(chi_done, 1)
            layer_norm(0)
            attention(L0)
            layer_norm(1)
            for t in range(NT):
                act.wait_ge(lo_mx, t + 1)
                act.activation(lg[:, (t % 2) * 8:(t % 2) * 8 + 8], lg[:, (t % 2) * 8:(t % 2) * 8 + 8], ACT.Exp,
                               bias=lmx[:, t % 2:t % 2 + 1], accum_out=lsum[:, t % 2:t % 2 + 1]).then_inc(lo_exp, 1)
                act.wait_ge(lo_tr, t + 1)
                if t >= 1:
                    act.wait_ge(lo_y, t)
                copy(tT[0][:, 0, :], bank[2][:, 0:P]).then_inc(lo_thi, 1)
            layer_norm(2)
            attention(L1)
            layer_norm(3)
            with act.Fori(0, 2) as half:
                for m in range(MT):
                    act.wait_ge(ff_g, half * MT + (m + 1))
                    act.activation(sig[m % 2], bank[4 + m % 2][:, :], ACT.Sigmoid).then_inc(ff_sig, 1)
                    act.wait_ge(ff_h, half * MT + (m + 1))
                    copy(hT[m % 2][0][:, 0, :], hidden[m % 2]).then_inc(ff_hhi, 1)

        @block.vector
        def _(dve):
            def low(out, in_, hi):
                return dve.tensor_tensor(out, in_, hi.bitcast(F32), ALU.subtract)

            def layer_norm(n):
                for t in range(NT):
                    dve.bn_stats(stats[:, 6 * t:6 * t + 6], xt[:, t, :]).then_inc(ln_stats, 1)
                for t in range(NT):
                    dve.wait_ge(ln_stats, n * NT + t + 1)
                    dve.bn_aggr(moments[:, 2 * t:2 * t + 2], stats[:, 6 * t:6 * t + 6]).then_inc(ln_moments, 1)
                dve.wait_ge(ln_rstd, n + 1)
                for t in range(NT + 1):
                    if t < NT:
                        if t >= 2:
                            dve.wait_ge(ln_t, n * NT + t - 1)
                        dve.tensor_scalar(xn[t % 2], xt[:, t, :], moments[:, 2 * t:2 * t + 1], rstd[:, t:t + 1],
                                          ALU.subtract, ALU.mult).then_inc(ln_xn, 1)
                    if t >= 1:
                        j = t - 1
                        dve.wait_ge(ln_hi, n * NT + j + 1)
                        low(xT[1][:, :, j * P:(j + 1) * P],
                            bank[6 + j % 2][:, :].rearrange("p (k n) -> p k n", k=KC),
                            xT[0][:, :, j * P:(j + 1) * P]).then_inc(ln_lo, 1)

            def attention(L):
                s = attn_sems[L.name]
                hd = L.hd

                def kv_low(g, b):
                    dve.wait_ge(s.vhi_done, count(g, b, 1, 1))
                    ps = bank[7]
                    vw = [flat(w)[:, 0:2 * hd].rearrange("p (t n) -> p t n", t=2) for w in v[b % VS]]
                    low(vw[1], ps[:, 0:2 * L.kvw].rearrange("p (t n) -> p t n", t=2)[:, :, hd:L.kvw],
                        vw[0]).then_inc(s.vlo_done, 1)
                    if L.normed:
                        dve.wait_ge(s.kr_done, count(g, b, 1, 1))
                    for i in range(2):
                        out, k_rows = kn[:, i * hd:(i + 1) * hd], ps[:, i * L.kvw:i * L.kvw + hd]
                        if L.normed:
                            dve.tensor_scalar(out, k_rows, kr[:, 2 * (b % 2) + i:2 * (b % 2) + i + 1], None,
                                              ALU.mult).then_inc(s.kn_done, 1)
                        else:
                            dve.tensor_copy(out, k_rows).then_inc(s.kn_done, 1)

                def k_low(g, b):
                    dve.wait_ge(s.khi_done, count(g, b, 1, 1))
                    ps = bank[7][0:hd, 0:KV]
                    hi, lo = (w[0:hd, 0, :] for w in kT[b % 2])
                    if L.normed:
                        dve.scalar_tensor_tensor(lo, ps, qkw[:, 2:3], hi.bitcast(F32),
                                                 ALU.mult, ALU.subtract).then_inc(s.klo_done, 1)
                    else:
                        low(lo, ps, hi).then_inc(s.klo_done, 1)

                def qt_low(g, b):
                    dve.wait_ge(s.qthi_done, count(g, b, 1, 1))
                    low(flat(qT[b % 2][1])[0:hd, :], bank[6][0:hd, :], flat(qT[b % 2][0])[0:hd, :]
                        ).then_inc(s.qlo_done, 1)

                def row_max(g, b):
                    if L.normed:
                        dve.wait_ge(s.rq_done, count(g, b, 1, 1))
                    for i in range(2):
                        pr = slice(2 * i, 2 * i + 2)
                        dve.wait_ge(s.s_done, count(g, b, 2, i + 1))
                        dve.tensor_reduce(mx[:, pr], bank[i][:, :].rearrange("p (h n) -> p h n", h=2), AX.X, ALU.max
                                          ).then_inc(s.mx_done, 1)
                        dve.wait_ge(s.mx_done, count(g, b, 2, i + 1))
                        if L.normed:
                            r = NH * (b % 2) + 2 * i
                            dve.scalar_tensor_tensor(nb[:, pr], mx[:, pr], -1.0, rq[:, r:r + 2], ALU.mult,
                                                     ALU.mult).then_inc(s.nb_done, 1)
                        else:
                            dve.tensor_scalar(nb[:, pr], mx[:, pr], -float(hd) ** -0.5, None, ALU.mult
                                              ).then_inc(s.nb_done, 1)

                def normalize(g, b):
                    for i in range(2):
                        pr = slice(2 * i, 2 * i + 2)
                        dve.wait_ge(s.exp_done, count(g, b, NH, 2 * i + 2))
                        dve.reciprocal(rs[:, pr], sums[:, pr]).then_inc(s.rs_done, 1)
                        dve.wait_ge(s.rs_done, count(g, b, 2, i + 1))
                        for h in (2 * i, 2 * i + 1):
                            dve.tensor_scalar(probs[:, h, :], probs[:, h, :], rs[:, h:h + 1], None, ALU.mult
                                              ).then_inc(s.pn_done, 1)

                def turn_low(g, b):
                    for kt in range(2):
                        dve.wait_ge(s.pthi_done, count(g, b, 2, kt + 1))
                        low(pT[1][:, kt, :], bank[2 + kt][:, :], pT[0][:, kt, :]).then_inc(s.ptlo_done, 1)

                def o_low(g, b):
                    dve.wait_ge(s.ohi_done, count(g, b, 1, 1))
                    low(flat(oT[1])[0:hd, :], bank[4][0:hd, :], flat(oT[0])[0:hd, :]).then_inc(s.olo_done, 1)

                def y_add(g, b):
                    dve.wait_ge(s.y_done, count(g, b, 1, 1))
                    dve.scalar_tensor_tensor(xt[:, b, :], bank[5][:, :], tg[:, L.gate:L.gate + 1], xt[:, b, :],
                                             ALU.mult, ALU.add).then_inc(s.yadd_done, 1)

                def body(g, first, last):
                    for b in range(NT):
                        ahead = not last or b + 2 < NT
                        turn_low(g, b)
                        if ahead:
                            kv_low(g, b + 2)
                        o_low(g, b)
                        if not last or b + 1 < NT:
                            row_max(g, b + 1)
                            normalize(g, b + 1)
                        if ahead:
                            k_low(g, b + 2)
                        y_add(g, b)
                        if ahead:
                            qt_low(g, b + 2)

                for b in range(2):
                    kv_low(0, b)
                    k_low(0, b)
                    qt_low(0, b)
                row_max(0, 0)
                normalize(0, 0)
                groups(dve, L, body)
                dve.wait_ge(s.yadd_done, L.groups * NT)

            dve.wait_ge(in_small, 80)
            dve.scalar_tensor_tensor(qkw[:, 2:3], qkw[:, 0:1], float(L0.hd) ** 0.5, qkw[:, 1:2], ALU.mult, ALU.mult
                                     ).then_inc(qkw_done, 1)
            dve.wait_ge(tanh_done, 1)
            dve.tensor_scalar(tg_lora[:, :], tg[:, 2:3], LORA_GAIN, None, ALU.mult).then_inc(gate_done, 1)
            dve.wait_ge(in_x, 16)
            dve.wait_ge(in_ctx, 16)
            for k in range(KC):
                dve.wait_ge(chi_done, k + 1)
                low(cT[1][:, k, :], craw[:, k, :], cT[0][:, k, :]).then_inc(clo_done, 1)
            dve.wait_ge(clo_done, KC)
            dve.wait_ge(qkw_done, 1)
            dve.wait_ge(gate_done, 1)
            layer_norm(0)
            attention(L0)
            layer_norm(1)
            for t in range(NT + 1):
                if t < NT:
                    dve.wait_ge(lo_p, t + 1)
                    ps = bank[6 + t % 2]
                    l8 = lg[:, (t % 2) * 8:(t % 2) * 8 + 8]
                    dve.tensor_tensor(l8, ps[:, P:136], bias_r[:, :], ALU.add).then_inc(lo_lg, 1)
                    dve.wait_ge(lo_lg, t + 1)
                    dve.tensor_reduce(lmx[:, t % 2:t % 2 + 1], l8, AX.X, ALU.max, negate=True).then_inc(lo_mx, 1)
                    dve.wait_ge(lo_exp, t + 1)
                    dve.reciprocal(lrs[:, t % 2:t % 2 + 1], lsum[:, t % 2:t % 2 + 1]).then_inc(lo_rs, 1)
                    dve.wait_ge(lo_rs, t + 1)
                    dve.tensor_scalar(l8, l8, lrs[:, t % 2:t % 2 + 1], None, ALU.mult).then_inc(lo_sc, 1)
                    dve.wait_ge(lo_sc, t + 1)
                    dve.tensor_tensor(lora_act[t % 2].rearrange("p (h r) -> p h r", h=EXPERTS),
                                      ps[:, 0:P].rearrange("p (h r) -> p h r", h=EXPERTS),
                                      l8.rearrange("p (h r) -> p h r", r=1).to_broadcast([P, EXPERTS, RANK]),
                                      ALU.mult).then_inc(lo_t, 1)
                    dve.wait_ge(lo_thi, t + 1)
                    low(tT[1][:, 0, :], bank[2][:, 0:P], tT[0][:, 0, :]).then_inc(lo_tlo, 1)
                if t >= 1:
                    n = t - 1
                    dve.wait_ge(lo_y, n + 1)
                    dve.scalar_tensor_tensor(xt[:, n, :], bank[4 + n % 2][:, :], tg_lora[:, 0:1], xt[:, n, :],
                                             ALU.mult, ALU.add).then_inc(lo_add, 1)
            dve.wait_ge(lo_add, NT)
            layer_norm(2)
            attention(L1)
            layer_norm(3)
            with dve.Fori(0, 2) as half:
                for m in range(MT + 1):
                    if m < MT:
                        dve.wait_ge(ff_sig, half * MT + (m + 1))
                        dve.tensor_tensor(gated[m % 2], bank[4 + m % 2][:, :], sig[m % 2], ALU.mult
                                          ).then_inc(ff_gated, 1)
                        dve.wait_ge(ff_gated, half * MT + (m + 1))
                        dve.wait_ge(ff_u, half * MT + (m + 1))
                        dve.tensor_tensor(hidden[m % 2], bank[6 + m % 2][:, :], gated[m % 2], ALU.mult
                                          ).then_inc(ff_h, 1)
                        dve.wait_ge(ff_hhi, half * MT + (m + 1))
                        low(hT[m % 2][1][:, 0, :], hidden[m % 2], hT[m % 2][0][:, 0, :]).then_inc(ff_hlo, 1)
                dve.wait_ge(ff_acc, half * MT + MT)
                for t in range(NB):
                    tile = x[:, bass.ds(half * (NB * D) + t * D, D)]
                    dve.scalar_tensor_tensor(tile, bank[t][:, :], tg[:, 3:4], tile, ALU.mult, ALU.add
                                             ).then_inc(ff_add, 1)

        @block.gpsimd
        def _(pool):
            def layer_norm(n):
                pool.wait_ge(ln_moments, n * NT + NT)
                pool.tensor_scalar(var_e[:, :], moments[:, 1:2 * NT:2], LN_EPS, None, ALU.add).then_inc(ln_vareps, 1)
                pool.wait_ge(ln_vareps, n + 1)
                pool.tensor_tensor(rstd[:, :], var_e[:, :], half_neg[:, 0:NT], ALU.pow).then_inc(ln_rstd, 1)

            def attention(L):
                s = attn_sems[L.name]
                hd = L.hd

                def split_chunk(raw_part, hi, lo, hi_sem, lo_sem, value):
                    pool.wait_ge(hi_sem, value)
                    pool.tensor_tensor(lo, raw_part, hi.bitcast(F32), ALU.subtract).then_inc(lo_sem, 1)

                def split_q(g, k):
                    sl = slice(k * L.qw, (k + 1) * L.qw)
                    split_chunk(raw_q[:, sl], flat(wq[0])[:, sl], flat(wq[1])[:, sl], s.wq_hi, s.wq_lo,
                                g * KC + (k + 1))

                def split_kv(g):
                    for i in range(2):
                        sl = slice(i * 2 * L.kvw, (i + 1) * 2 * L.kvw)
                        split_chunk(raw_kv[:, sl], flat(wkv[0])[:, sl], flat(wkv[1])[:, sl], s.wkv_hi, s.wkv_lo,
                                    g * 2 + (i + 1))

                def split_o(g):
                    for h in range(NH):
                        split_chunk(rawo(L)[:, h, :], wo[0][0:hd, h, :], wo[1][0:hd, h, :], s.wo_hi, s.wo_lo,
                                    g * NH + (h + 1))

                def k_norm(g, b):
                    c = slice(2 * (b % 2), 2 * (b % 2) + 2)
                    pool.wait_ge(s.ksq_done, count(g, b, 2, 2))
                    pool.tensor_tensor(kvar[:, c], ksum[:, c], hd_eps[:, 0:2], ALU.add).then_inc(s.kvar_done, 1)
                    pool.wait_ge(s.kvar_done, count(g, b, 1, 1))
                    pool.tensor_tensor(kr[:, c], kvar[:, c], half_neg[:, 0:2], ALU.pow).then_inc(s.kr_done, 1)

                def q_norm(g, b):
                    c = slice(NH * (b % 2), NH * (b % 2) + NH)
                    pool.wait_ge(s.qsq_done, count(g, b, NH, NH))
                    pool.tensor_tensor(qvar[:, c], qsum[:, c], hd_eps[:, :], ALU.add).then_inc(s.qvar_done, 1)
                    pool.wait_ge(s.qvar_done, count(g, b, 1, 1))
                    pool.tensor_tensor(rq[:, c], qvar[:, c], half_neg[:, 0:NH], ALU.pow).then_inc(s.rq_done, 1)

                def body(g, first, last):
                    for b in range(NT):
                        ahead = not last or b + 2 < NT
                        crossing = b + 2 == NT - 1 and not last
                        if b == 0 and not first:
                            split_o(g)
                        if ahead and L.normed:
                            k_norm(g, b + 2)
                        if crossing:
                            split_kv(g + 1)
                        if ahead and L.normed:
                            q_norm(g, b + 2)
                        if crossing:
                            for k in range(KC):
                                split_q(g + 1, k)

                split_kv(0)
                for k in range(KC):
                    split_q(0, k)
                split_o(0)
                if L.normed:
                    for b in range(2):
                        k_norm(0, b)
                        q_norm(0, b)
                groups(pool, L, body)

            pool.memset(ident[:, :], 0.0).then_inc(ident_zero, 1)
            pool.memset(half_neg[:, :], -0.5).then_inc(consts, 1)
            pool.memset(hd_eps[:, :], RMS_EPS * L0.hd).then_inc(consts, 1)
            pool.wait_ge(ident_zero, 1)
            pool.affine_select(out=ident[:, :], in_=ident[:, :], compare_op=ALU.not_equal, fill=1.0, base=0,
                               pattern=[[-1, P]], channel_multiplier=1).then_inc(consts, 1)
            pool.wait_ge(consts, 3)
            layer_norm(0)
            attention(L0)
            layer_norm(1)
            pool.wait_ge(in_lora, 32)
            for i, (r, w, n) in enumerate(((raw_q, lw, KC * 136), (raw_kv, lb, D))):
                whi, wlo = (t.rearrange("p k n -> p (k n)") for t in w)
                pool.wait_ge(attn_sems["a"].y_done, L0.groups * NT)
                pool.tensor_copy(whi, r[:, 0:n]).then_inc(lw_hi, 1)
                pool.wait_ge(lw_hi, i + 1)
                pool.tensor_tensor(wlo, r[:, 0:n], whi.bitcast(F32), ALU.subtract).then_inc(lw_lo, 1)
            layer_norm(2)
            pool.wait_ge(lo_y, NT)
            attention(L1)
            pool.wait_ge(attn_sems["c"].y_done, L1.groups * NT)
            for w, name in ((fgate, "gate_t"), (fup, "up_t"), (fdown, "down_t")):
                pool.dma_start(w, a[name].rearrange("(k p) n -> p k n", p=P)).then_inc(in_ffw, 16)
            layer_norm(3)


def kernel(**inputs):
    import numpy as _np
    import concourse.bacc as _bacc
    from concourse import mybir as _mybir
    from concourse.bass_utils import run_bass_kernel_spmd as _run

    i = {k: _np.asarray(v) for k, v in inputs.items()}
    laid = {
        "x": i["x"].reshape(TOK, D),
        "ctx_t": i["ctx_4096"].reshape(TOK, D).T,
        "g_xattn": i["g_xattn"], "g_ffn": i["g_ffn"],
        "q_norm_w": i["L0_xattn_q_norm_w"], "k_norm_w": i["L0_xattn_k_norm_w"],
        "wq_a": i["L0_xattn_Wq"], "wk_a": i["L0_xattn_Wk"], "wv_a": i["L0_xattn_Wv"], "wo_a": i["L0_xattn_Wo"],
        "lora_w": _np.concatenate([i["L0_ffn_A"].reshape(EXPERTS * RANK, D), i["L0_ffn_Wr"]], axis=0).T,
        "lora_b": i["L0_ffn_B"].transpose(0, 2, 1).reshape(EXPERTS * RANK, D),
        "lora_bias": i["L0_ffn_br"],
        "wq_c": i["L1_xattn_Wq"].T, "wk_c": i["L1_xattn_Wk"].T, "wv_c": i["L1_xattn_Wv"].T,
        "wo_c": i["L1_xattn_Wo"].T,
        "gate_t": i["L1_ffn_W_gate"].T, "up_t": i["L1_ffn_W_up"].T, "down_t": i["L1_ffn_W_down"].T,
    }
    nc = _bacc.Bacc("TRN2", target_bir_lowering=False, num_devices=1)
    arrays, args = {}, {}
    for name, v in laid.items():
        v = _np.ascontiguousarray(v)
        arrays[f"in_{name}"] = v
        args[name] = nc.dram_tensor(f"in_{name}", v.shape, _mybir.dt.from_np(v.dtype), kind="ExternalInput").ap()
    args["out"] = nc.dram_tensor("out_0", (TOK, D), _mybir.dt.float32, kind="ExternalOutput").ap()
    build(nc, args)
    r = _run(nc, [arrays], core_ids=[0])
    return r.results[0]["out_0"].reshape(BATCH, SEQ, D)
```

```python
from contextlib import ExitStack

import concourse.bass as bass
from concourse import mybir

F32 = mybir.dt.float32
F32R = mybir.dt.float32r
ALU = mybir.AluOpType
ACT = mybir.ActivationFunctionType
AX = mybir.AxisListType

P = 128
BATCH, SEQ, D = 8, 128, 512
KC = D // P
NT = BATCH
TOK = BATCH * SEQ
NH = 4
NB = 4
HALF = NB * SEQ
VS = 4
KV = 2 * SEQ
EARLY = 2
LN_EPS = 1e-5
RMS_EPS = 1e-6
EXPERTS, RANK = 8, 16
LW = P + EXPERTS
LORA_GAIN = EXPERTS * 2.0
FF = 1792
MT = FF // P
MH = MT // 2
MD = 3
CS = 4
SPLIT = 37376


class Layer:

    def __init__(self, name, groups, head_dim, normed, gate):
        self.name, self.groups, self.hd, self.normed, self.gate = name, groups, head_dim, normed, gate
        self.qw = NH * head_dim
        self.kvw = 2 * head_dim
        self.oc = self.qw // P
        self.op = 1 if head_dim == P else 1 + self.oc
        self.tiles = groups * NT


L0 = Layer("a", 8, 128, True, 0)
L1 = Layer("c", 4, 96, False, 1)


class AttentionSems:

    def __init__(self, sem):
        self.in_q = sem("in_q")
        self.in_kv = sem("in_kv")
        self.in_o = sem("in_o")
        self.wq_hi = sem("wq_hi")
        self.wq_lo = sem("wq_lo")
        self.wkv_hi = sem("wkv_hi")
        self.wkv_lo = sem("wkv_lo")
        self.wo_hi = sem("wo_hi")
        self.wo_lo = sem("wo_lo")
        self.kv_done = sem("kv_done")
        self.ksq_done = sem("ksq_done")
        self.kvar_done = sem("kvar_done")
        self.kr_done = sem("kr_done")
        self.vhi_done = sem("vhi_done")
        self.vlo_done = sem("vlo_done")
        self.kn_done = sem("kn_done")
        self.kt_done = sem("kt_done")
        self.khi_done = sem("khi_done")
        self.klo_done = sem("klo_done")
        self.q_done = sem("q_done")
        self.qsq_done = sem("qsq_done")
        self.qvar_done = sem("qvar_done")
        self.rq_done = sem("rq_done")
        self.qcp_done = sem("qcp_done")
        self.qt_done = sem("qt_done")
        self.qthi_done = sem("qthi_done")
        self.qlo_done = sem("qlo_done")
        self.s_done = sem("s_done")
        self.mx_done = sem("mx_done")
        self.nb_done = sem("nb_done")
        self.exp_done = sem("exp_done")
        self.rs_done = sem("rs_done")
        self.pn_done = sem("pn_done")
        self.t_done = sem("t_done")
        self.pthi_done = sem("pthi_done")
        self.ptlo_done = sem("ptlo_done")
        self.pv_done = sem("pv_done")
        self.ohi_done = sem("ohi_done")
        self.olo_done = sem("olo_done")
        self.y_done = sem("y_done")
        self.yadd_done = sem("yadd_done")


class NormSems:

    def __init__(self, sem):
        self.stats = sem("stats")
        self.moments = sem("moments")
        self.vareps = sem("vareps")
        self.rstd = sem("rstd")
        self.xn = sem("xn")
        self.turned = sem("turned")
        self.hi = sem("hi")
        self.lo = sem("lo")


def count(g, b, per_tile, more):
    return g * (NT * per_tile) + (b * per_tile + more)


def later(L, g, b, n):
    if isinstance(g, int) and g == L.groups - 1 and b + n >= NT:
        return (L1, 0, b + n - NT) if L is L0 else None
    return (L, g, b + n)


def is_at(L, g, layer, group):
    return L is layer and isinstance(g, int) and g == group


def beside(L, g, b):
    norm = finish = None
    if is_at(L, g, L0, 0) and b + EARLY + 1 < NT:
        norm = (0, b + EARLY + 1)
    if is_at(L, g, L0, L0.groups - 1):
        norm = (1, b - 1) if b >= 1 else None
        finish = b - 2 if b >= 2 else None
    if is_at(L, g, L1, 0):
        norm = (1, NT - 1) if b == 0 else None
        finish = NT - 2 + b if b < 2 else None
    if is_at(L, g, L1, L1.groups - 1):
        norm = (3, b - 1) if b >= 1 else None
    return norm, finish


def build(nc, a):
    with ExitStack() as ctx:
        def sb(name, n, dt=F32):
            return ctx.enter_context(nc.sbuf_tensor(name, [P, n], dt))

        def sem(name):
            return ctx.enter_context(nc.semaphore(name))

        split = sb("split", SPLIT, F32R)
        spot = [0]

        def take(n):
            spot[0] += n
            return split[:, spot[0] - n:spot[0]]

        def chunks(ap, n):
            return ap.rearrange("p (k n) -> p k n", k=n)

        def pair(n, k):
            return chunks(take(n), k), chunks(take(n), k)

        def flat(w):
            return w.rearrange("p k n -> p (k n)")

        xT = pair(KC * TOK, KC)
        context_at = spot[0]
        cT = pair(KC * TOK, KC)
        wo_at = spot[0]
        wo = pair(NH * D, NH)
        v = [pair(2 * P, 2) for _ in range(VS)]
        oT = pair(NH * P, NH)
        pT_at = spot[0]
        pT = pair(2 * NH * P, 2)
        kT = [pair(KV, 1) for _ in range(2)]
        qT = [pair(NH * P, NH) for _ in range(2)]
        wq_at = spot[0]
        wq = pair(KC * NH * P, KC)
        wkv = pair(KC * 2 * P, KC)
        lw = pair(KC * LW, KC)
        lb = pair(D, 1)
        tT = pair(P, 1)
        assert spot[0] <= SPLIT

        spot[0] = context_at
        fgate = chunks(take(KC * FF), KC)
        spot[0] = wq_at
        fup = chunks(take(KC * FF), KC)
        fdown_first = chunks(take(MD * D), MD)
        assert spot[0] <= SPLIT
        spot[0] = wo_at
        fdown_rest = chunks(take((MT - MD) * D), MT - MD)
        assert spot[0] <= pT_at
        spot[0] = pT_at
        hT = [pair(HALF, 1) for _ in range(2)]

        x = sb("x", NT * D)
        xt = chunks(x[:, :], NT)
        craw = sb("craw", CS * KC * P)
        raw = sb("raw", 5120)
        raw_q = raw[:, 0:2048]
        raw_kv = raw[:, 2048:3072]
        raw_o = raw[:, 3072:5120]
        scratch = sb("scratch", 3840)
        probs = chunks(scratch[:, 0:1024], NH)
        qn = scratch[:, 1024:1536]
        kn = scratch[:, 1536:1792]
        sink = [scratch[:, 1792 + P * i:1792 + P * (i + 1)] for i in range(6)]
        xn = [scratch[:, 2560 + 512 * i:3072 + 512 * i] for i in range(2)]
        lora_act = [scratch[:, 3584 + P * i:3584 + P * (i + 1)] for i in range(2)]
        sig = [scratch[:, 0 + 512 * i:512 + 512 * i] for i in range(2)]
        gated = [scratch[:, 1024 + 512 * i:1536 + 512 * i] for i in range(2)]
        hidden = [scratch[:, 2048 + 512 * i:2560 + 512 * i] for i in range(2)]

        ident = sb("ident", P)
        half_neg = sb("half_neg", NH)
        gates = sb("gates", 4)
        tg = sb("tg", 4)
        tg_lora = sb("tg_lora", 1)
        qkw = sb("qkw", 3)
        bias_r = sb("bias_r", EXPERTS)
        stats = sb("stats", NT * 6)
        moments = sb("moments", NT * 2)
        var_e = sb("var_e", NT)
        rstd = sb("rstd", NT)
        ksum = sb("ksum", 4)
        kvar = sb("kvar", 4)
        kr = sb("kr", 4)
        qsum = sb("qsum", 8)
        qvar = sb("qvar", 8)
        rq = sb("rq", 8)
        hd_eps = sb("hd_eps", 4)
        mx = sb("mx", NH)
        nb = sb("nb", NH)
        sums = sb("sums", NH)
        rs = sb("rs", NH)
        lg = sb("lg", 2 * EXPERTS)
        lmx = sb("lmx", 2)
        lsum = sb("lsum", 2)
        lrs = sb("lrs", 2)

        bank = [ctx.enter_context(nc.psum_tensor(f"bank{i}", [P, 512], F32)) for i in range(8)]

        def norm_bank(n, t):
            if n == 3 and t >= NT - 3:
                return 7 if t == NT - 1 else 6
            return 4 if n == 2 or (n == 0 and t in (0, EARLY)) else 5

        def context_slot(t):
            return chunks(craw[:, (t % CS) * KC * P:(t % CS + 1) * KC * P], KC)

        def xn_slot(n, t):
            return n - 1 if n in (1, 2) else t % 2

        in_x, in_x_rest = sem("in_x"), sem("in_x_rest")
        in_ctx = [sem(f"in_ctx{i}") for i in range(CS)]
        in_small, in_lora = sem("in_small"), sem("in_lora")
        in_ff_first, in_ff_second, in_down_first, in_down_rest = (
            sem(f"in_{n}") for n in ("ff_first", "ff_second", "down_first", "down_rest"))
        ident_zero, consts = sem("ident_zero"), sem("consts")
        tanh_done, gate_done, qkw_done = sem("tanh_done"), sem("gate_done"), sem("qkw_done")
        ctx_hi, ctx_lo = sem("ctx_hi"), sem("ctx_lo")
        norm = [NormSems(lambda what, n=n: sem(f"norm{n}_{what}")) for n in range(4)]
        attn = {L.name: AttentionSems(lambda what, L=L: sem(f"{L.name}_{what}")) for L in (L0, L1)}
        lw_hi, lw_lo = sem("lw_hi"), sem("lw_lo")
        lora_proj, lora_logits, lora_max, lora_exp = (sem(f"lora_{n}") for n in ("proj", "logits", "max", "exp"))
        lora_rsum, lora_prob, lora_scaled, lora_turned = (
            sem(f"lora_{n}") for n in ("rsum", "prob", "scaled", "turned"))
        lora_hi, lora_lo, lora_out, lora_added = (sem(f"lora_{n}") for n in ("hi", "lo", "out", "added"))
        ff_gate, ff_sig, ff_up, ff_gated, ff_hidden = (
            sem(f"ff_{n}") for n in ("gate", "sig", "up", "gated", "hidden"))
        ff_hi, ff_lo, ff_down, ff_free = (sem(f"ff_{n}") for n in ("hi", "lo", "down", "free"))
        out_done = sem("out_done")

        def q_src(L, g):
            w = a["wq_" + L.name].rearrange("(k p) n -> p k n", p=P)
            return w[:, :, bass.ds(g * L.qw, L.qw)]

        def load_context(eng, t):
            src = a["ctx_t"].rearrange("(k p) n -> p k n", p=P)
            eng.dma_start(context_slot(t), src[:, :, t * P:(t + 1) * P]).then_inc(in_ctx[t % CS], 16)

        def kv_src(L, g):
            w = a["wkv_" + L.name].rearrange("(k p) n -> p k n", p=P)
            return w[:, :, bass.ds(g * L.kvw, L.kvw)]

        def o_src(L, g):
            w = a["wo_" + L.name].rearrange("(n p) m -> p n m", p=P)
            return w[:, bass.ds(g * L.oc, L.oc), :]

        def rawq(L):
            return chunks(raw_q[:, 0:KC * L.qw], KC)

        def rawkv(L):
            return chunks(raw_kv[:, 0:KC * L.kvw], KC)

        def rawo(L):
            return chunks(raw_o[:, 0:L.oc * D], L.oc)

        def v_parts(L, b):
            return [chunks(flat(w)[:, 0:2 * L.hd], 2) for w in v[b % VS]]

        def head_moves(L):
            if L.op == 1:
                return [(slice(0, P), slice(0, NH), slice(0, P), slice(0, NH * P))]
            rest = P - L.hd
            return [(slice(0, L.hd), slice(0, L.oc), slice(0, L.hd), slice(0, L.oc * P))] + [
                (slice(L.hd, P), slice(j, j + 1), slice(rest * j, rest * (j + 1)), slice(L.oc * P, NH * P))
                for j in range(L.oc)]

        block = ctx.enter_context(nc.Block())

        def layer(eng, L, step):
            for b in range(NT):
                step(L, 0, b)
            with eng.Fori(1, L.groups - 1) as g:
                for b in range(NT):
                    step(L, g, b)
            for b in range(NT):
                step(L, L.groups - 1, b)

        @block.sync
        def _(sp):
            x_src = a["x"].rearrange("(t p) d -> p t d", p=P)
            out_dst = a["out"].rearrange("(t p) d -> p t d", p=P)

            def load_q(L, g):
                sp.dma_start(rawq(L), q_src(L, g)).then_inc(attn[L.name].in_q, 16)

            def load_kv(L, g):
                sp.dma_start(rawkv(L), kv_src(L, g)).then_inc(attn[L.name].in_kv, 16)

            def load_o(L, g):
                sp.dma_start(rawo(L), o_src(L, g)).then_inc(attn[L.name].in_o, 16)

            def next_groups(L):
                s = attn[L.name]
                with sp.Fori(1, L.groups) as g:
                    sp.wait_ge(s.wq_lo, g * KC)
                    load_q(L, g)
                    sp.wait_ge(s.wkv_lo, g * 2)
                    load_kv(L, g)
                    sp.wait_ge(s.wo_lo, g * L.oc)
                    load_o(L, g)

            sp.dma_start(xt[:, 0:EARLY, :], x_src[:, 0:EARLY, :]).then_inc(in_x, 16)
            load_kv(L0, 0)
            load_q(L0, 0)
            for t in range(EARLY, CS):
                load_context(sp, t)
            for n, name in enumerate(("g_xattn", "g_ffn")):
                sp.dma_start(gates[:, 2 * n:2 * n + 2], a[name].partition_broadcast(P)).then_inc(in_small, 16)
            for n, name in enumerate(("q_norm_w", "k_norm_w")):
                sp.dma_start(qkw[:, n:n + 1], a[name].rearrange("(p a) -> p a", a=1)).then_inc(in_small, 16)
            sp.dma_start(bias_r[:, :], a["lora_bias"].partition_broadcast(P)).then_inc(in_small, 16)
            sp.dma_start(xt[:, EARLY:NT, :], x_src[:, EARLY:NT, :]).then_inc(in_x_rest, 16)
            load_o(L0, 0)
            for t in range(CS, NT):
                sp.wait_ge(ctx_lo, t - CS + 1)
                load_context(sp, t)
            next_groups(L0)
            s = attn[L0.name]
            sp.wait_ge(s.wq_lo, L0.groups * KC)
            sp.wait_ge(s.wkv_lo, L0.groups * 2)
            sp.dma_start(chunks(raw_q[:, 0:KC * LW], KC),
                         a["lora_w"].rearrange("(k p) n -> p k n", p=P)).then_inc(in_lora, 16)
            sp.dma_start(raw_kv[:, 0:D], a["lora_b"]).then_inc(in_lora, 16)
            sp.wait_ge(lw_lo, 2)
            load_kv(L1, 0)
            load_q(L1, 0)
            sp.wait_ge(s.wo_lo, L0.groups * L0.oc)
            load_o(L1, 0)
            next_groups(L1)
            sp.wait_ge(ff_free, 2 * NB)
            sp.dma_start(out_dst[:, 0:NB, :], xt[:, 0:NB, :]).then_inc(out_done, 16)
            for t in range(NB, NT):
                sp.wait_ge(ff_free, NB + t + 1)
                sp.dma_start(out_dst[:, t, :], xt[:, t, :]).then_inc(out_done, 16)
            sp.wait_ge(out_done, 16 * (1 + NT - NB))

        @block.tensor
        def _(pe):
            def mm3(out, w, m, start=False, stop=False):
                whi, wlo = w
                mhi, mlo = m
                pe.matmul(out, whi, mhi, start=start, stop=False)
                pe.matmul(out, whi, mlo, start=False, stop=False)
                return pe.matmul(out, wlo, mhi, start=False, stop=stop)

            def at(pr, *idx):
                return tuple(t[idx] for t in pr)

            def cols(w, k, n):
                return tuple(flat(t)[:, k * n:(k + 1) * n] for t in w)

            def tile_of(src, k, t):
                return at(src, slice(None), k, slice(t * P, (t + 1) * P))

            def awake(n):
                for _ in range(n):
                    pe.transpose(bank[0][:, 0:P], ident[:, :], ident[:, :])

            def norm_turn(n, t):
                pe.wait_ge(norm[n].xn, t + 1)
                if n == 0 and t >= 2:
                    pe.wait_ge(norm[0].lo, t - 1)
                if n == 3 and t == NT - 2:
                    pe.wait_ge(norm[3].lo, t)
                b = bank[norm_bank(n, t)]
                for k in range(KC):
                    last = pe.transpose(b[:, k * P:(k + 1) * P], xn[xn_slot(n, t)][:, k * P:(k + 1) * P], ident[:, :])
                last.then_inc(norm[n].turned, 1)

            def kv_proj(L, g, b, between=None):
                s = attn[L.name]
                gb, tile = g + b // NT, b % NT
                if b > 0 or not isinstance(g, int) or g > 0:
                    pe.wait_ge(s.klo_done, count(g, b, 1, 0))
                elif L is L1:
                    pe.wait_ge(attn[L0.name].klo_done, L0.tiles)
                for i, src in enumerate((cT, xT)):
                    if i == 1 and between is not None:
                        between()
                    if is_at(L, g, L0, 0) and b < NT:
                        pe.wait_ge((ctx_lo, norm[0].lo)[i], tile + 1)
                    if is_at(L, g, L1, 0) and b < NT:
                        pe.wait_ge(norm[2].lo, tile + 1)
                    out = bank[7][:, i * L.kvw:(i + 1) * L.kvw]
                    for k in range(KC):
                        if tile == 0 and i == 0 and k % 2 == 0:
                            pe.wait_ge(s.wkv_lo, gb * 2 + (k // 2 + 1))
                        last = mm3(out, tile_of(src, k, tile), cols(wkv, k, L.kvw), start=k == 0, stop=k == KC - 1)
                last.then_inc(s.kv_done, 1)

            def q_proj(L, g, b):
                s = attn[L.name]
                gb, tile = g + b // NT, b % NT
                if b > 0 or not isinstance(g, int) or g > 0:
                    pe.wait_ge(s.qlo_done, count(g, b, 1, 0))
                elif L is L1:
                    pe.wait_ge(attn[L0.name].qlo_done, L0.tiles)
                for k in range(KC):
                    if tile == 0:
                        pe.wait_ge(s.wq_lo, gb * KC + (k + 1))
                    last = mm3(bank[6][:, 0:L.qw], tile_of(xT, k, tile), cols(wq, k, L.qw),
                               start=k == 0, stop=k == KC - 1)
                last.then_inc(s.q_done, 1)

            def k_turn(L, g, b):
                s = attn[L.name]
                pe.wait_ge(s.kn_done, count(g, b, 2, 2))
                for i in range(2):
                    last = pe.transpose(bank[7][0:L.hd, i * P:(i + 1) * P], kn[:, i * L.hd:(i + 1) * L.hd],
                                        ident[:, :])
                last.then_inc(s.kt_done, 1)

            def q_turn(L, g, b):
                s = attn[L.name]
                pe.wait_ge(s.qcp_done, count(g, b, 1, 1))
                if L.normed:
                    pe.wait_ge(s.qsq_done, count(g, b, NH, NH))
                for h in range(NH):
                    last = pe.transpose(bank[6][0:L.hd, h * P:(h + 1) * P], qn[:, h * L.hd:(h + 1) * L.hd],
                                        ident[:, :])
                last.then_inc(s.qt_done, 1)

            def scores(L, g, b):
                s = attn[L.name]
                pe.wait_ge(s.klo_done, count(g, b, 1, 1))
                pe.wait_ge(s.qlo_done, count(g, b, 1, 1))
                for h in range(NH):
                    last = mm3(bank[h // 2][:, (h % 2) * KV:(h % 2 + 1) * KV],
                               at(qT[b % 2], slice(0, L.hd), h, slice(None)),
                               at(kT[b % 2], slice(0, L.hd), 0, slice(None)), start=True, stop=True)
                    if h % 2:
                        last.then_inc(s.s_done, 1)

            def turn(L, g, b):
                s = attn[L.name]
                for i in range(2):
                    pe.wait_ge(s.pn_done, count(g, b, NH, 2 * i + 2))
                    for kt in range(2):
                        for h in (2 * i, 2 * i + 1):
                            last = pe.transpose(bank[2 + kt][:, h * P:(h + 1) * P],
                                                probs[:, h, kt * P:(kt + 1) * P], ident[:, :])
                        if i == 1:
                            last.then_inc(s.t_done, 1)

            def values(L, g, b):
                s = attn[L.name]
                if is_at(L, g, L1, 0) and b == 2:
                    pe.wait_ge(norm[2].lo, NT)
                for kt in range(2):
                    pe.wait_ge(s.ptlo_done, count(g, b, 2, kt + 1))
                    last = mm3(bank[4][0:L.hd, :],
                               tuple(flat(w)[:, kt * L.hd:(kt + 1) * L.hd] for w in v[b % VS]),
                               at(pT, slice(None), kt, slice(None)), start=kt == 0, stop=kt == 1)
                last.then_inc(s.pv_done, 1)

            def project(L, g, b):
                s = attn[L.name]
                before, finish = beside(L, g, b)
                pe.wait_ge(s.olo_done, count(g, b, L.op, L.op))
                if before is not None and norm_bank(*before) == 5:
                    pe.wait_ge(norm[before[0]].lo, before[1] + 1)
                if finish is not None:
                    pe.wait_ge(lora_added, finish + 1)
                if b > 0 or not isinstance(g, int) or g > 0:
                    pe.wait_ge(s.yadd_done, count(g, b, 1, 0))
                elif L is L1:
                    pe.wait_ge(attn[L0.name].yadd_done, L0.tiles)
                for c in range(L.oc):
                    if b == 0:
                        pe.wait_ge(s.wo_lo, g * L.oc + (c + 1))
                    last = mm3(bank[5][:, :], at(oT, slice(None), c, slice(None)),
                               at(wo, slice(None), c, slice(None)), start=c == 0, stop=c == L.oc - 1)
                last.then_inc(s.y_done, 1)

            def lora_project(t):
                if t >= 1:
                    pe.wait_ge(norm[2].lo, t)
                pe.wait_ge(norm[1].lo, t + 1)
                pe.wait_ge(lw_lo, 2)
                for k in range(KC):
                    last = mm3(bank[4][:, 0:LW], tile_of(xT, k, t), at(lw, slice(None), k, slice(None)),
                               start=k == 0, stop=k == KC - 1)
                last.then_inc(lora_proj, 1)

            def lora_turn(L, g, b, t):
                if L is L0:
                    pe.wait_ge(attn[L0.name].yadd_done, count(g, b, 1, 0))
                else:
                    pe.wait_ge(attn[L0.name].yadd_done, L0.tiles)
                    if b > 0:
                        pe.wait_ge(attn[L1.name].yadd_done, b)
                pe.wait_ge(lora_scaled, t + 1)
                pe.transpose(bank[5][:, 0:P], lora_act[t % 2], ident[:, :]
                             ).then_inc(lora_turned, 1)

            def lora_project_out(t):
                pe.wait_ge(lora_lo, t + 1)
                mm3(bank[5][:, :], at(tT, slice(None), 0, slice(None)),
                    at(lb, slice(None), 0, slice(None)), start=True, stop=True).then_inc(lora_out, 1)

            def step(L, g, b):
                beside_norm, finish = beside(L, g, b)
                one, two = later(L, g, b, 1), later(L, g, b, 2)
                turn(L, g, b)
                if two is not None:
                    kv_proj(*two, between=None if finish is None else lambda: lora_turn(L, g, b, finish))
                values(L, g, b)
                if finish is not None:
                    lora_project_out(finish)
                if beside_norm is not None and beside_norm[0] == 3:
                    norm_turn(*beside_norm)
                if one is not None:
                    scores(*one)
                if beside_norm is not None and beside_norm[0] < 3:
                    if finish is not None:
                        pe.wait_ge(lora_added, finish + 1)
                    norm_turn(*beside_norm)
                if two is not None:
                    q_proj(*two)
                    k_turn(*two)
                if finish is not None:
                    pe.wait_ge(attn[L.name].olo_done, count(g, b, L.op, L.op))
                    norm_turn(2, finish)
                project(L, g, b)
                if beside_norm is not None and beside_norm[0] == 1:
                    lora_project(beside_norm[1])
                if two is not None:
                    q_turn(*two)

            pe.wait_ge(consts, 3)
            awake(22)
            norm_turn(0, 0)
            norm_turn(0, 1)
            awake(10)
            kv_proj(L0, 0, 0)
            q_proj(L0, 0, 0)
            k_turn(L0, 0, 0)
            q_turn(L0, 0, 0)
            scores(L0, 0, 0)
            norm_turn(0, 2)
            kv_proj(L0, 0, 1)
            q_proj(L0, 0, 1)
            k_turn(L0, 0, 1)
            q_turn(L0, 0, 1)
            layer(pe, L0, step)
            layer(pe, L1, step)
            awake(18)
            norm_turn(3, NT - 1)

            pe.wait_ge(norm[3].lo, NB)
            with pe.Fori(0, 2) as half:
                toks = bass.ds(half * HALF, HALF)

                def down(m):
                    pe.wait_ge(in_down_first if m < MD else in_down_rest, 16)
                    pe.wait_ge(ff_lo, half * MT + (m + 1))
                    w = fdown_first[:, m, :] if m < MD else fdown_rest[:, m - MD, :]
                    for t in range(NB):
                        if m == 0:
                            pe.wait_ge(ff_free, half * NB + (t + 1))
                        for i, part in enumerate(hT[m % 2]):
                            last = pe.matmul(bank[t][:, :], part[:, 0, t * P:(t + 1) * P], w,
                                             start=m == 0 and i == 0, stop=m == MT - 1 and i == 1)
                        if m == MT - 1:
                            last.then_inc(ff_down, 1)

                for m in range(MT):
                    pe.wait_ge(in_ff_first if m < MH else in_ff_second, 32)
                    if m < 2:
                        pe.wait_ge(norm[3].lo, NT - 1 + m)
                    for w, bk, done in ((fgate, 4, ff_gate), (fup, 6, ff_up)):
                        if m >= 2:
                            pe.wait_ge(ff_hidden, half * MT + (m - 1))
                        for k in range(KC):
                            for i, part in enumerate(xT):
                                last = pe.matmul(bank[bk + m % 2][:, :], w[:, k, m * P:(m + 1) * P],
                                                 part[:, k, toks],
                                                 start=k == 0 and i == 0, stop=k == KC - 1 and i == 1)
                        last.then_inc(done, 1)
                    if m >= 1:
                        down(m - 1)
                down(MT - 1)

        @block.scalar
        def _(act):
            def copy(out, in_):
                return act.activation(out, in_, ACT.Copy)

            def norm_hi(n, t):
                act.wait_ge(norm[n].turned, t + 1)
                copy(xT[0][:, :, t * P:(t + 1) * P], chunks(bank[norm_bank(n, t)][:, :], KC)
                     ).then_inc(norm[n].hi, 1)

            def context_hi(t):
                act.wait_ge(in_ctx[t % CS], 16 * (t // CS + 1))
                copy(cT[0][:, :, t * P:(t + 1) * P], context_slot(t)).then_inc(ctx_hi, 1)

            def kv_evac(L, g, b):
                s, hd = attn[L.name], L.hd
                act.wait_ge(s.kv_done, count(g, b, 1, 1))
                ps = bank[7]
                if L.normed:
                    for i in range(2):
                        act.activation(sink[i], ps[:, i * L.kvw:i * L.kvw + hd], ACT.Square,
                                       accum_out=ksum[:, 2 * (b % 2) + i:2 * (b % 2) + i + 1]
                                       ).then_inc(s.ksq_done, 1)
                copy(v_parts(L, b)[0], chunks(ps[:, 0:2 * L.kvw], 2)[:, :, hd:L.kvw]).then_inc(s.vhi_done, 1)

            def q_evac(L, g, b):
                s, hd = attn[L.name], L.hd
                act.wait_ge(s.q_done, count(g, b, 1, 1))
                copy(qn[:, 0:L.qw], bank[6][:, 0:L.qw]).then_inc(s.qcp_done, 1)
                if L.normed:
                    for h in range(NH):
                        act.activation(sink[2 + h], bank[6][:, h * hd:(h + 1) * hd], ACT.Square,
                                       accum_out=qsum[:, NH * (b % 2) + h:NH * (b % 2) + h + 1]
                                       ).then_inc(s.qsq_done, 1)

            def k_evac(L, g, b):
                s = attn[L.name]
                act.wait_ge(s.kt_done, count(g, b, 1, 1))
                out, ps = kT[b % 2][0][0:L.hd, 0, :], bank[7][0:L.hd, 0:KV]
                if L.normed:
                    act.activation(out, ps, ACT.Copy, scale=qkw[:, 2:3]).then_inc(s.khi_done, 1)
                else:
                    copy(out, ps).then_inc(s.khi_done, 1)

            def qt_evac(L, g, b):
                s = attn[L.name]
                act.wait_ge(s.qt_done, count(g, b, 1, 1))
                copy(flat(qT[b % 2][0])[0:L.hd, :], bank[6][0:L.hd, :]).then_inc(s.qthi_done, 1)

            def exps(L, g, b):
                s = attn[L.name]
                for h in range(NH):
                    if h % 2 == 0:
                        act.wait_ge(s.nb_done, count(g, b, 2, h // 2 + 1))
                    scale = rq[:, NH * (b % 2) + h:NH * (b % 2) + h + 1] if L.normed else float(L.hd) ** -0.5
                    act.activation(probs[:, h, :], bank[h // 2][:, (h % 2) * KV:(h % 2 + 1) * KV], ACT.Exp,
                                   bias=nb[:, h:h + 1], scale=scale,
                                   accum_out=sums[:, h:h + 1]).then_inc(s.exp_done, 1)

            def turn_evac(L, g, b):
                s = attn[L.name]
                for kt in range(2):
                    act.wait_ge(s.t_done, count(g, b, 2, kt + 1))
                    copy(pT[0][:, kt, :], bank[2 + kt][:, :]).then_inc(s.pthi_done, 1)

            def o_evac(L, g, b):
                s = attn[L.name]
                act.wait_ge(s.pv_done, count(g, b, 1, 1))
                for rows, cs, prows, pcols in head_moves(L):
                    copy(oT[0][rows, cs, :], chunks(bank[4][prows, pcols], cs.stop - cs.start)
                         ).then_inc(s.ohi_done, 1)

            def kv_hi(L, g, i):
                s = attn[L.name]
                act.wait_ge(s.in_kv, g * 16 + 16)
                sl = slice(i * 2 * L.kvw, (i + 1) * 2 * L.kvw)
                copy(flat(wkv[0])[:, sl], raw_kv[:, sl]).then_inc(s.wkv_hi, 1)

            def q_hi(L, g, k):
                s = attn[L.name]
                act.wait_ge(s.in_q, g * 16 + 16)
                sl = slice(k * L.qw, (k + 1) * L.qw)
                copy(flat(wq[0])[:, sl], raw_q[:, sl]).then_inc(s.wq_hi, 1)

            def o_hi(L, g, c):
                s = attn[L.name]
                act.wait_ge(s.in_o, g * 16 + 16)
                copy(wo[0][:, c, :], rawo(L)[:, c, :]).then_inc(s.wo_hi, 1)

            def lora_weight_hi():
                act.wait_ge(in_lora, 32)
                copy(flat(lw[0]), raw_q[:, 0:KC * LW]).then_inc(lw_hi, 1)
                copy(flat(lb[0]), raw_kv[:, 0:D]).then_inc(lw_hi, 1)

            def lora_act_hi(t):
                act.wait_ge(lora_turned, t + 1)
                copy(tT[0][:, 0, :], bank[5][:, 0:P]).then_inc(lora_hi, 1)

            def router_exp(t):
                l8 = lg[:, (t % 2) * EXPERTS:(t % 2 + 1) * EXPERTS]
                act.wait_ge(lora_max, t + 1)
                act.activation(l8, l8, ACT.Exp, bias=lmx[:, t % 2:t % 2 + 1],
                               accum_out=lsum[:, t % 2:t % 2 + 1]).then_inc(lora_exp, 1)

            def step(L, g, b):
                beside_norm, finish = beside(L, g, b)
                one, two = later(L, g, b, 1), later(L, g, b, 2)
                new_kvq = later(L, g, NT - 1, 1) if b == NT - 3 else None
                new_q = later(L, g, NT - 1, 1) if b == NT - 2 else None
                new_o = b == 0 and not is_at(L, g, L0, 0)

                def group_of(n):
                    return n[0], n[1] + n[2] // NT

                turn_evac(L, g, b)
                if new_o:
                    if is_at(L, g, L1, 0):
                        act.wait_ge(attn[L0.name].y_done, L0.tiles)
                    else:
                        act.wait_ge(attn[L.name].y_done, count(g, 0, 1, 0))
                    o_hi(L, g, 0)
                    o_hi(L, g, 1)
                if new_q is not None:
                    q_hi(*group_of(new_q), 2)
                    q_hi(*group_of(new_q), 3)
                if is_at(L, g, L0, L0.groups - 1) and b == 1:
                    lora_weight_hi()
                if finish is not None:
                    lora_act_hi(finish)
                if two is not None:
                    kv_evac(*two)
                if new_kvq is not None:
                    kv_hi(*group_of(new_kvq), 0)
                if new_o:
                    o_hi(L, g, 2)
                o_evac(L, g, b)
                if is_at(L, g, L0, 0) and b + EARLY + 1 < NT:
                    context_hi(b + EARLY + 1)
                if new_kvq is not None:
                    kv_hi(*group_of(new_kvq), 1)
                if new_o and L.oc > 3:
                    o_hi(L, g, 3)
                if beside_norm is not None:
                    norm_hi(*beside_norm)
                if one is not None:
                    exps(*one)
                if finish is not None:
                    norm_hi(2, finish)
                if two is not None:
                    q_evac(*two)
                    k_evac(*two)
                if new_kvq is not None:
                    q_hi(*group_of(new_kvq), 0)
                    q_hi(*group_of(new_kvq), 1)
                if two is not None:
                    qt_evac(*two)
                if beside_norm is not None and beside_norm[0] == 1:
                    router_exp(beside_norm[1])

            for t in range(EARLY):
                load_context(act, t)
            kv_hi(L0, 0, 0)
            kv_hi(L0, 0, 1)
            context_hi(0)
            norm_hi(0, 0)
            norm_hi(0, 1)
            context_hi(1)
            for k in range(KC):
                q_hi(L0, 0, k)
            kv_evac(L0, 0, 0)
            q_evac(L0, 0, 0)
            k_evac(L0, 0, 0)
            qt_evac(L0, 0, 0)
            context_hi(2)
            norm_hi(0, 2)
            exps(L0, 0, 0)
            kv_evac(L0, 0, 1)
            for c in range(L0.oc):
                o_hi(L0, 0, c)
            q_evac(L0, 0, 1)
            act.wait_ge(in_small, 80)
            act.activation(tg[:, :], gates[:, :], ACT.Tanh).then_inc(tanh_done, 1)
            k_evac(L0, 0, 1)
            qt_evac(L0, 0, 1)
            layer(act, L0, step)
            layer(act, L1, step)
            norm_hi(3, NT - 1)
            with act.Fori(0, 2) as half:
                for m in range(MT):
                    act.wait_ge(ff_gate, half * MT + (m + 1))
                    act.activation(sig[m % 2], bank[4 + m % 2][:, :], ACT.Sigmoid).then_inc(ff_sig, 1)
                    act.wait_ge(ff_hidden, half * MT + (m + 1))
                    copy(hT[m % 2][0][:, 0, :], hidden[m % 2]).then_inc(ff_hi, 1)

        @block.vector
        def _(dve):
            def low(out, in_, hi):
                return dve.tensor_tensor(out, in_, hi.bitcast(F32), ALU.subtract)

            def norm_stats(n, t):
                if n == 0:
                    dve.wait_ge(in_x if t < EARLY else in_x_rest, 16)
                elif n == 1:
                    dve.wait_ge(attn[L0.name].yadd_done, L0.tiles - NT + t + 1)
                elif n == 2:
                    dve.wait_ge(lora_added, t + 1)
                else:
                    dve.wait_ge(attn[L1.name].yadd_done, L1.tiles - NT + t + 1)
                dve.bn_stats(stats[:, 6 * t:6 * t + 6], xt[:, t, :]).then_inc(norm[n].stats, 1)
                dve.wait_ge(norm[n].stats, t + 1)
                dve.bn_aggr(moments[:, 2 * t:2 * t + 2], stats[:, 6 * t:6 * t + 6]).then_inc(norm[n].moments, 1)

            def norm_scale(n, t):
                dve.wait_ge(norm[n].rstd, t + 1)
                if n in (1, 2) and t >= 1:
                    dve.wait_ge(norm[n].turned, t)
                if n in (0, 3) and t >= 2:
                    dve.wait_ge(norm[n].turned, t - 1)
                dve.tensor_scalar(xn[xn_slot(n, t)], xt[:, t, :], moments[:, 2 * t:2 * t + 1], rstd[:, t:t + 1],
                                  ALU.subtract, ALU.mult).then_inc(norm[n].xn, 1)

            def norm_low(n, t):
                sl = slice(t * P, (t + 1) * P)
                dve.wait_ge(norm[n].hi, t + 1)
                low(xT[1][:, :, sl], chunks(bank[norm_bank(n, t)][:, :], KC), xT[0][:, :, sl]
                    ).then_inc(norm[n].lo, 1)

            def context_low(t):
                sl = slice(t * P, (t + 1) * P)
                dve.wait_ge(ctx_hi, t + 1)
                low(cT[1][:, :, sl], context_slot(t), cT[0][:, :, sl]).then_inc(ctx_lo, 1)

            def kv_low(L, g, b):
                s, hd = attn[L.name], L.hd
                dve.wait_ge(s.vhi_done, count(g, b, 1, 1))
                ps = bank[7]
                vhi, vlo = v_parts(L, b)
                low(vlo, chunks(ps[:, 0:2 * L.kvw], 2)[:, :, hd:L.kvw], vhi).then_inc(s.vlo_done, 1)
                if L.normed:
                    dve.wait_ge(s.kr_done, count(g, b, 1, 1))
                for i in range(2):
                    out, k_rows = kn[:, i * hd:(i + 1) * hd], ps[:, i * L.kvw:i * L.kvw + hd]
                    if L.normed:
                        dve.tensor_scalar(out, k_rows, kr[:, 2 * (b % 2) + i:2 * (b % 2) + i + 1], None,
                                          ALU.mult).then_inc(s.kn_done, 1)
                    else:
                        dve.tensor_copy(out, k_rows).then_inc(s.kn_done, 1)

            def k_low(L, g, b):
                s = attn[L.name]
                dve.wait_ge(s.khi_done, count(g, b, 1, 1))
                ps = bank[7][0:L.hd, 0:KV]
                hi, lo = (w[0:L.hd, 0, :] for w in kT[b % 2])
                if L.normed:
                    dve.scalar_tensor_tensor(lo, ps, qkw[:, 2:3], hi.bitcast(F32),
                                             ALU.mult, ALU.subtract).then_inc(s.klo_done, 1)
                else:
                    low(lo, ps, hi).then_inc(s.klo_done, 1)

            def qt_low(L, g, b):
                s = attn[L.name]
                dve.wait_ge(s.qthi_done, count(g, b, 1, 1))
                low(flat(qT[b % 2][1])[0:L.hd, :], bank[6][0:L.hd, :], flat(qT[b % 2][0])[0:L.hd, :]
                    ).then_inc(s.qlo_done, 1)

            def row_max(L, g, b, i):
                s = attn[L.name]
                pr = slice(2 * i, 2 * i + 2)
                dve.wait_ge(s.s_done, count(g, b, 2, i + 1))
                dve.tensor_reduce(mx[:, pr], chunks(bank[i][:, :], 2), AX.X, ALU.max).then_inc(s.mx_done, 1)
                dve.wait_ge(s.mx_done, count(g, b, 2, i + 1))
                if L.normed:
                    r = NH * (b % 2) + 2 * i
                    dve.wait_ge(s.rq_done, count(g, b, 1, 1))
                    dve.scalar_tensor_tensor(nb[:, pr], mx[:, pr], -1.0, rq[:, r:r + 2], ALU.mult,
                                             ALU.mult).then_inc(s.nb_done, 1)
                else:
                    dve.tensor_scalar(nb[:, pr], mx[:, pr], -float(L.hd) ** -0.5, None, ALU.mult
                                      ).then_inc(s.nb_done, 1)

            def normalize(L, g, b):
                s = attn[L.name]
                for i in range(2):
                    pr = slice(2 * i, 2 * i + 2)
                    dve.wait_ge(s.exp_done, count(g, b, NH, 2 * i + 2))
                    dve.reciprocal(rs[:, pr], sums[:, pr]).then_inc(s.rs_done, 1)
                    dve.wait_ge(s.rs_done, count(g, b, 2, i + 1))
                    for h in (2 * i, 2 * i + 1):
                        dve.tensor_scalar(probs[:, h, :], probs[:, h, :], rs[:, h:h + 1], None, ALU.mult
                                          ).then_inc(s.pn_done, 1)

            def turn_low(L, g, b):
                s = attn[L.name]
                for kt in range(2):
                    dve.wait_ge(s.pthi_done, count(g, b, 2, kt + 1))
                    low(pT[1][:, kt, :], bank[2 + kt][:, :], pT[0][:, kt, :]).then_inc(s.ptlo_done, 1)

            def o_low(L, g, b):
                s = attn[L.name]
                for rows, cs, prows, pcols in head_moves(L):
                    dve.wait_ge(s.ohi_done, count(g, b, L.op, L.op))
                    low(oT[1][rows, cs, :], chunks(bank[4][prows, pcols], cs.stop - cs.start),
                        oT[0][rows, cs, :]).then_inc(s.olo_done, 1)

            def y_add(L, g, b):
                s = attn[L.name]
                dve.wait_ge(s.y_done, count(g, b, 1, 1))
                dve.scalar_tensor_tensor(xt[:, b, :], bank[5][:, :], tg[:, L.gate:L.gate + 1], xt[:, b, :],
                                         ALU.mult, ALU.add).then_inc(s.yadd_done, 1)

            def router_logits(t):
                l8 = lg[:, (t % 2) * EXPERTS:(t % 2 + 1) * EXPERTS]
                dve.wait_ge(lora_proj, t + 1)
                dve.tensor_tensor(l8, bank[4][:, P:LW], bias_r[:, :], ALU.add).then_inc(lora_logits, 1)
                dve.wait_ge(lora_logits, t + 1)
                dve.tensor_reduce(lmx[:, t % 2:t % 2 + 1], l8, AX.X, ALU.max, negate=True).then_inc(lora_max, 1)

            def lora_scale(t):
                l8 = lg[:, (t % 2) * EXPERTS:(t % 2 + 1) * EXPERTS]
                dve.wait_ge(lora_exp, t + 1)
                dve.reciprocal(lrs[:, t % 2:t % 2 + 1], lsum[:, t % 2:t % 2 + 1]).then_inc(lora_rsum, 1)
                dve.wait_ge(lora_rsum, t + 1)
                dve.tensor_scalar(l8, l8, lrs[:, t % 2:t % 2 + 1], None, ALU.mult).then_inc(lora_prob, 1)
                dve.wait_ge(lora_prob, t + 1)
                dve.tensor_tensor(lora_act[t % 2].rearrange("p (h r) -> p h r", h=EXPERTS),
                                  bank[4][:, 0:P].rearrange("p (h r) -> p h r", h=EXPERTS),
                                  l8.rearrange("p (h r) -> p h r", r=1).to_broadcast([P, EXPERTS, RANK]),
                                  ALU.mult).then_inc(lora_scaled, 1)

            def lora_low(t):
                dve.wait_ge(lora_hi, t + 1)
                low(tT[1][:, 0, :], bank[5][:, 0:P], tT[0][:, 0, :]).then_inc(lora_lo, 1)

            def lora_add(t):
                dve.wait_ge(lora_out, t + 1)
                dve.scalar_tensor_tensor(xt[:, t, :], bank[5][:, :], tg_lora[:, 0:1], xt[:, t, :],
                                         ALU.mult, ALU.add).then_inc(lora_added, 1)

            def step(L, g, b):
                beside_norm, finish = beside(L, g, b)
                one, two = later(L, g, b, 1), later(L, g, b, 2)
                next_norm = beside(*one)[0] if one is not None else None
                turn_low(L, g, b)
                if beside_norm is not None:
                    norm_scale(*beside_norm)
                if finish is not None:
                    lora_low(finish)
                if two is not None:
                    kv_low(*two)
                if finish is not None:
                    lora_add(finish)
                if one is not None:
                    row_max(*one, 0)
                if finish is not None:
                    norm_stats(2, finish)
                o_low(L, g, b)
                if is_at(L, g, L0, 0) and b + EARLY + 1 < NT:
                    context_low(b + EARLY + 1)
                if beside_norm is not None and beside_norm[0] == 3:
                    norm_low(*beside_norm)
                if one is not None:
                    row_max(*one, 1)
                if finish is not None:
                    norm_scale(2, finish)
                if beside_norm is not None and beside_norm[0] < 3:
                    norm_low(*beside_norm)
                if one is not None:
                    normalize(*one)
                if finish is not None:
                    norm_low(2, finish)
                if two is not None:
                    k_low(*two)
                y_add(L, g, b)
                if beside_norm is not None and beside_norm[0] == 1:
                    router_logits(beside_norm[1])
                if next_norm is not None:
                    norm_stats(*next_norm)
                if two is not None:
                    qt_low(*two)
                if beside_norm is not None and beside_norm[0] == 1:
                    lora_scale(beside_norm[1])

            s = attn[L0.name]
            norm_stats(0, 0)
            norm_stats(0, 1)
            norm_scale(0, 0)
            norm_scale(0, 1)
            for i in range(2):
                sl = slice(i * 2 * L0.kvw, (i + 1) * 2 * L0.kvw)
                dve.wait_ge(s.wkv_hi, i + 1)
                low(flat(wkv[1])[:, sl], raw_kv[:, sl], flat(wkv[0])[:, sl]).then_inc(s.wkv_lo, 1)
            context_low(0)
            norm_low(0, 0)
            norm_low(0, 1)
            context_low(1)
            for k in range(KC):
                sl = slice(k * L0.qw, (k + 1) * L0.qw)
                dve.wait_ge(s.wq_hi, k + 1)
                low(flat(wq[1])[:, sl], raw_q[:, sl], flat(wq[0])[:, sl]).then_inc(s.wq_lo, 1)
            dve.wait_ge(in_small, 80)
            dve.scalar_tensor_tensor(qkw[:, 2:3], qkw[:, 0:1], float(L0.hd) ** 0.5, qkw[:, 1:2], ALU.mult, ALU.mult
                                     ).then_inc(qkw_done, 1)
            dve.wait_ge(qkw_done, 1)
            kv_low(L0, 0, 0)
            k_low(L0, 0, 0)
            norm_stats(0, 2)
            qt_low(L0, 0, 0)
            norm_scale(0, 2)
            row_max(L0, 0, 0, 0)
            context_low(2)
            row_max(L0, 0, 0, 1)
            norm_low(0, 2)
            normalize(L0, 0, 0)
            kv_low(L0, 0, 1)
            k_low(L0, 0, 1)
            dve.wait_ge(tanh_done, 1)
            dve.tensor_scalar(tg_lora[:, :], tg[:, 2:3], LORA_GAIN, None, ALU.mult).then_inc(gate_done, 1)
            qt_low(L0, 0, 1)
            dve.wait_ge(gate_done, 1)
            norm_stats(0, EARLY + 1)
            layer(dve, L0, step)
            layer(dve, L1, step)
            norm_stats(3, NT - 1)
            norm_scale(3, NT - 1)
            norm_low(3, NT - 1)
            dve.tensor_copy(lmx[:, 0:1], lmx[:, 1:2]).then_inc(ff_free, NB)
            with dve.Fori(0, 2) as half:
                for m in range(MT):
                    dve.wait_ge(ff_sig, half * MT + (m + 1))
                    dve.tensor_tensor(gated[m % 2], bank[4 + m % 2][:, :], sig[m % 2], ALU.mult
                                      ).then_inc(ff_gated, 1)
                    dve.wait_ge(ff_gated, half * MT + (m + 1))
                    dve.wait_ge(ff_up, half * MT + (m + 1))
                    dve.tensor_tensor(hidden[m % 2], bank[6 + m % 2][:, :], gated[m % 2], ALU.mult
                                      ).then_inc(ff_hidden, 1)
                    dve.wait_ge(ff_hi, half * MT + (m + 1))
                    low(hT[m % 2][1][:, 0, :], hidden[m % 2], hT[m % 2][0][:, 0, :]).then_inc(ff_lo, 1)
                for t in range(NB):
                    dve.wait_ge(ff_down, half * NB + (t + 1))
                    tile = x[:, bass.ds(half * (NB * D) + t * D, D)]
                    dve.scalar_tensor_tensor(tile, bank[t][:, :], tg[:, 3:4], tile, ALU.mult, ALU.add
                                             ).then_inc(ff_free, 1)

        @block.gpsimd
        def _(pool):
            def norm_rstd(n, t):
                pool.wait_ge(norm[n].moments, t + 1)
                pool.tensor_scalar(var_e[:, t:t + 1], moments[:, 2 * t + 1:2 * t + 2], LN_EPS, None, ALU.add
                                   ).then_inc(norm[n].vareps, 1)
                pool.wait_ge(norm[n].vareps, t + 1)
                pool.tensor_tensor(rstd[:, t:t + 1], var_e[:, t:t + 1], half_neg[:, 0:1], ALU.pow
                                   ).then_inc(norm[n].rstd, 1)

            def part_low(lo, raw_part, hi):
                return pool.tensor_tensor(lo, raw_part, hi.bitcast(F32), ALU.subtract)

            def kv_lo(L, g, i):
                s = attn[L.name]
                sl = slice(i * 2 * L.kvw, (i + 1) * 2 * L.kvw)
                pool.wait_ge(s.wkv_hi, g * 2 + (i + 1))
                part_low(flat(wkv[1])[:, sl], raw_kv[:, sl], flat(wkv[0])[:, sl]).then_inc(s.wkv_lo, 1)

            def q_lo(L, g, k):
                s = attn[L.name]
                sl = slice(k * L.qw, (k + 1) * L.qw)
                pool.wait_ge(s.wq_hi, g * KC + (k + 1))
                part_low(flat(wq[1])[:, sl], raw_q[:, sl], flat(wq[0])[:, sl]).then_inc(s.wq_lo, 1)

            def o_lo(L, g, c):
                s = attn[L.name]
                pool.wait_ge(s.wo_hi, g * L.oc + (c + 1))
                part_low(wo[1][:, c, :], rawo(L)[:, c, :], wo[0][:, c, :]).then_inc(s.wo_lo, 1)

            def k_norm(L, g, b):
                s = attn[L.name]
                c = slice(2 * (b % 2), 2 * (b % 2) + 2)
                pool.wait_ge(s.ksq_done, count(g, b, 2, 2))
                pool.tensor_tensor(kvar[:, c], ksum[:, c], hd_eps[:, 0:2], ALU.add).then_inc(s.kvar_done, 1)
                pool.wait_ge(s.kvar_done, count(g, b, 1, 1))
                pool.tensor_tensor(kr[:, c], kvar[:, c], half_neg[:, 0:2], ALU.pow).then_inc(s.kr_done, 1)

            def q_norm(L, g, b):
                s = attn[L.name]
                c = slice(NH * (b % 2), NH * (b % 2) + NH)
                pool.wait_ge(s.qsq_done, count(g, b, NH, NH))
                pool.tensor_tensor(qvar[:, c], qsum[:, c], hd_eps[:, :], ALU.add).then_inc(s.qvar_done, 1)
                pool.wait_ge(s.qvar_done, count(g, b, 1, 1))
                pool.tensor_tensor(rq[:, c], qvar[:, c], half_neg[:, 0:NH], ALU.pow).then_inc(s.rq_done, 1)

            def lora_weight_lo():
                for i, (r, w, n) in enumerate(((raw_q, lw, KC * LW), (raw_kv, lb, D))):
                    pool.wait_ge(lw_hi, i + 1)
                    part_low(flat(w[1]), r[:, 0:n], flat(w[0])).then_inc(lw_lo, 1)

            def step(L, g, b):
                beside_norm, finish = beside(L, g, b)
                two = later(L, g, b, 2)
                new_kvq = later(L, g, NT - 1, 1) if b == NT - 3 else None
                new_q = later(L, g, NT - 1, 1) if b == NT - 2 else None
                new_o = b == 0 and not is_at(L, g, L0, 0)

                def group_of(n):
                    return n[0], n[1] + n[2] // NT

                if new_o:
                    o_lo(L, g, 0)
                if new_q is not None:
                    q_lo(*group_of(new_q), 2)
                    q_lo(*group_of(new_q), 3)
                if beside_norm is not None:
                    norm_rstd(*beside_norm)
                if is_at(L, g, L1, L1.groups - 1) and b == NT - 2:
                    s = attn[L1.name]
                    gate_src, up_src = (a[n].rearrange("(k p) n -> p k n", p=P) for n in ("gate_t", "up_t"))
                    pool.wait_ge(s.kv_done, L1.tiles)
                    pool.wait_ge(s.q_done, L1.tiles)
                    for cols, done in ((slice(0, MH * P), in_ff_first), (slice(MH * P, FF), in_ff_second)):
                        pool.dma_start(fgate[:, :, cols], gate_src[:, :, cols]).then_inc(done, 16)
                        pool.dma_start(fup[:, :, cols], up_src[:, :, cols]).then_inc(done, 16)
                        if done is in_ff_first:
                            pool.dma_start(fdown_first, down_src[:, 0:MD, :]).then_inc(in_down_first, 16)
                if is_at(L, g, L0, L0.groups - 1) and b == 1:
                    lora_weight_lo()
                if two is not None and two[0].normed:
                    k_norm(*two)
                if new_kvq is not None:
                    kv_lo(*group_of(new_kvq), 0)
                    kv_lo(*group_of(new_kvq), 1)
                if new_o:
                    for c in range(1, L.oc):
                        o_lo(L, g, c)
                if finish is not None:
                    norm_rstd(2, finish)
                if two is not None and two[0].normed:
                    q_norm(*two)
                if new_kvq is not None:
                    q_lo(*group_of(new_kvq), 0)
                    q_lo(*group_of(new_kvq), 1)

            down_src = a["down_t"].rearrange("(m p) n -> p m n", p=P)
            pool.memset(ident[:, :], 0.0).then_inc(ident_zero, 1)
            pool.memset(half_neg[:, :], -0.5).then_inc(consts, 1)
            pool.memset(hd_eps[:, :], RMS_EPS * L0.hd).then_inc(consts, 1)
            pool.wait_ge(ident_zero, 1)
            pool.affine_select(out=ident[:, :], in_=ident[:, :], compare_op=ALU.not_equal, fill=1.0, base=0,
                               pattern=[[-1, P]], channel_multiplier=1).then_inc(consts, 1)
            pool.wait_ge(consts, 3)
            norm_rstd(0, 0)
            norm_rstd(0, 1)
            k_norm(L0, 0, 0)
            q_norm(L0, 0, 0)
            norm_rstd(0, 2)
            k_norm(L0, 0, 1)
            o_lo(L0, 0, 0)
            o_lo(L0, 0, 1)
            q_norm(L0, 0, 1)
            o_lo(L0, 0, 2)
            o_lo(L0, 0, 3)
            layer(pool, L0, step)
            layer(pool, L1, step)
            norm_rstd(3, NT - 1)
            pool.wait_ge(attn[L1.name].y_done, L1.tiles)
            pool.dma_start(fdown_rest, down_src[:, MD:MT, :]).then_inc(in_down_rest, 16)


def kernel(**inputs):
    import numpy as _np
    import concourse.bacc as _bacc
    from concourse import mybir as _mybir
    from concourse.bass_utils import run_bass_kernel_spmd as _run

    i = {k: _np.asarray(v) for k, v in inputs.items()}

    def by_group(L, wk, wv):
        k, v = (w.reshape(D, L.groups, L.hd) for w in (wk, wv))
        return _np.concatenate([k, v], axis=2).reshape(D, L.groups * L.kvw)

    wo_heads = i["L1_xattn_Wo"].T.reshape(L1.groups, NH, L1.hd, D)
    laid = {
        "x": i["x"].reshape(TOK, D),
        "ctx_t": i["ctx_4096"].reshape(TOK, D).T,
        "g_xattn": i["g_xattn"], "g_ffn": i["g_ffn"],
        "q_norm_w": i["L0_xattn_q_norm_w"], "k_norm_w": i["L0_xattn_k_norm_w"],
        "wq_a": i["L0_xattn_Wq"], "wkv_a": by_group(L0, i["L0_xattn_Wk"], i["L0_xattn_Wv"]), "wo_a": i["L0_xattn_Wo"],
        "lora_w": _np.concatenate([i["L0_ffn_A"].reshape(EXPERTS * RANK, D), i["L0_ffn_Wr"]], axis=0).T,
        "lora_b": i["L0_ffn_B"].transpose(0, 2, 1).reshape(EXPERTS * RANK, D),
        "lora_bias": i["L0_ffn_br"],
        "wq_c": i["L1_xattn_Wq"].T, "wkv_c": by_group(L1, i["L1_xattn_Wk"].T, i["L1_xattn_Wv"].T),
        "wo_c": _np.concatenate([
            wo_heads[:, 0:NH - 1], wo_heads[:, NH - 1].reshape(L1.groups, NH - 1, P - L1.hd, D)], axis=2
        ).reshape(L1.groups * L1.qw, D),
        "gate_t": i["L1_ffn_W_gate"].T, "up_t": i["L1_ffn_W_up"].T, "down_t": i["L1_ffn_W_down"].T,
    }
    nc = _bacc.Bacc("TRN2", target_bir_lowering=False, num_devices=1)
    arrays, args = {}, {}
    for name, v in laid.items():
        v = _np.ascontiguousarray(v)
        arrays[f"in_{name}"] = v
        args[name] = nc.dram_tensor(f"in_{name}", v.shape, _mybir.dt.from_np(v.dtype), kind="ExternalInput").ap()
    args["out"] = nc.dram_tensor("out_0", (TOK, D), _mybir.dt.float32, kind="ExternalOutput").ap()
    build(nc, args)
    r = _run(nc, [arrays], core_ids=[0])
    return r.results[0]["out_0"].reshape(BATCH, SEQ, D)
```
